# Optimizing a Trainium2 kernel written in Bass

```python
import numpy as np
import jax
import jax.numpy as jnp

def _softmax(x, axis=-1):
    return jax.nn.softmax(x, axis=axis)

def _gelu(x):
    return jax.nn.gelu(x, approximate=True)

def _silu(x):
    return jax.nn.silu(x)

def _sigmoid(x):
    return jax.nn.sigmoid(x)

def _layernorm(x, axis=-1, eps=1e-05):
    m = jnp.mean(x, axis=axis, keepdims=True)
    v = jnp.var(x, axis=axis, keepdims=True)
    return (x - m) / jnp.sqrt(v + eps)

def _scatter_add(tgt, idx, src, axis=0):
    return tgt.at[idx].add(src)

def _segment_sum(src, seg, n):
    return jax.ops.segment_sum(src, seg, n)
kernel_name = 'mk_seq_postln_d1_jaxref_r8_1948ad'

def setup_inputs(seed: int=0):
    np.random.seed(seed)
    _w = jnp.asarray

    def _L0_attn_setup():
        import jax, jax.numpy as jnp
        import numpy as np
        B, T, HM = (2, 256, 128)
        HEADS = 16
        DK = HM // 2 // HEADS
        DV = HM // HEADS
        LOW_RANK = 16
        GATE_NORM = 16.0
        EPS = 1e-05

        def _ln(x, w, b):
            m = x.mean(-1, keepdims=True)
            v = ((x - m) ** 2).mean(-1, keepdims=True)
            return (x - m) * jax.lax.rsqrt(v + EPS) * w + b

        def _rms(x, w):
            return x * jax.lax.rsqrt((x * x).mean(-1, keepdims=True) + EPS) * w

        def _gla(q, k, v, gk):

            def step(S, inp):
                qt, kt, vt, gt = inp
                S = jnp.exp(gt)[..., None] * S + kt[..., None] * vt[..., None, :]
                return (S, jnp.einsum('bhk,bhkv->bhv', qt, S))
            xs = tuple((jnp.moveaxis(a, 1, 0) for a in (q, k, v, gk)))
            S0 = jnp.zeros((q.shape[0], q.shape[2], q.shape[3], v.shape[3]), q.dtype)
            _, o = jax.lax.scan(step, S0, xs)
            return jnp.moveaxis(o, 0, 1)
        key = jax.random.key(seed)
        ks = jax.random.split(key, 12)

        def p(k, shape, s=0.02):
            return jax.random.normal(k, shape, jnp.float32) * s
        return dict(x=jax.random.normal(ks[0], (B, T, HM), jnp.float32), ln_w=jnp.ones((HM,), jnp.float32), ln_b=jnp.zeros((HM,), jnp.float32), Wq=p(ks[1], (HM, HEADS * DK)), Wk=p(ks[2], (HM, HEADS * DK)), Wv=p(ks[3], (HM, HEADS * DV)), gk_w1=p(ks[4], (HM, LOW_RANK)), gk_w2=p(ks[5], (LOW_RANK, HEADS * DK)), gk_b2=jnp.zeros((HEADS * DK,), jnp.float32), Wg=p(ks[6], (HM, HEADS * DV)), rms_w=jnp.ones((DV,), jnp.float32), Wo=p(ks[7], (HEADS * DV, HM)), W1=p(ks[8], (HM, 2 * HM)), b1=jnp.zeros((2 * HM,), jnp.float32), W2=p(ks[9], (2 * HM, HM)), b2=jnp.zeros((HM,), jnp.float32))
    _L0_attn_in = _L0_attn_setup()

    def _L0_ffn_setup():
        import jax, jax.numpy as jnp
        import numpy as np
        B, S, D, E, K = (4, 256, 128, 8, 2)
        H = 4 * D
        key = jax.random.key(seed)
        ks = jax.random.split(key, 4)
        sc = lambda n: 1.0 / np.sqrt(n)
        return {'x': jax.random.normal(ks[0], (B, S, D), jnp.float32), 'gate_w': jax.random.normal(ks[1], (D, E), jnp.float32) * sc(D), 'gate_b': jnp.zeros((E,), jnp.float32), 'w1': jax.random.normal(ks[2], (E, D, H), jnp.float32) * sc(D), 'b1': jnp.zeros((E, H), jnp.float32), 'w2': jax.random.normal(ks[3], (E, H, D), jnp.float32) * sc(H), 'b2': jnp.zeros((E, D), jnp.float32)}
    _L0_ffn_in = _L0_ffn_setup()
    _d = {'L0_attn_x': _L0_attn_in['x'], 'L0_attn_ln_w': _L0_attn_in['ln_w'], 'L0_attn_ln_b': _L0_attn_in['ln_b'], 'L0_attn_Wq': _L0_attn_in['Wq'], 'L0_attn_Wk': _L0_attn_in['Wk'], 'L0_attn_Wv': _L0_attn_in['Wv'], 'L0_attn_gk_w1': _L0_attn_in['gk_w1'], 'L0_attn_gk_w2': _L0_attn_in['gk_w2'], 'L0_attn_gk_b2': _L0_attn_in['gk_b2'], 'L0_attn_Wg': _L0_attn_in['Wg'], 'L0_attn_rms_w': _L0_attn_in['rms_w'], 'L0_attn_Wo': _L0_attn_in['Wo'], 'L0_attn_W1': _L0_attn_in['W1'], 'L0_attn_b1': _L0_attn_in['b1'], 'L0_attn_W2': _L0_attn_in['W2'], 'L0_attn_b2': _L0_attn_in['b2'], 'L0_ffn_gate_w': _L0_ffn_in['gate_w'], 'L0_ffn_gate_b': _L0_ffn_in['gate_b'], 'L0_ffn_w1': _L0_ffn_in['w1'], 'L0_ffn_b1': _L0_ffn_in['b1'], 'L0_ffn_w2': _L0_ffn_in['w2'], 'L0_ffn_b2': _L0_ffn_in['b2']}
    _x0 = _d['L0_attn_x']
    _d['L0_attn_x'] = jax.random.normal(jax.random.fold_in(jax.random.key(seed), 1), (32, 256, 128), dtype=_x0.dtype)
    del _x0
    return _d

def reference(L0_attn_x, L0_attn_ln_w, L0_attn_ln_b, L0_attn_Wq, L0_attn_Wk, L0_attn_Wv, L0_attn_gk_w1, L0_attn_gk_w2, L0_attn_gk_b2, L0_attn_Wg, L0_attn_rms_w, L0_attn_Wo, L0_attn_W1, L0_attn_b1, L0_attn_W2, L0_attn_b2, L0_ffn_gate_w, L0_ffn_gate_b, L0_ffn_w1, L0_ffn_b1, L0_ffn_w2, L0_ffn_b2):

    def _L0_attn_ref(x, ln_w, ln_b, Wq, Wk, Wv, gk_w1, gk_w2, gk_b2, Wg, rms_w, Wo, W1, b1, W2, b2):
        import jax, jax.numpy as jnp
        import numpy as np
        B, T, HM = (2, 256, 128)
        HEADS = 16
        DK = HM // 2 // HEADS
        DV = HM // HEADS
        LOW_RANK = 16
        GATE_NORM = 16.0
        EPS = 1e-05

        def _ln(x, w, b):
            m = x.mean(-1, keepdims=True)
            v = ((x - m) ** 2).mean(-1, keepdims=True)
            return (x - m) * jax.lax.rsqrt(v + EPS) * w + b

        def _rms(x, w):
            return x * jax.lax.rsqrt((x * x).mean(-1, keepdims=True) + EPS) * w

        def _gla(q, k, v, gk):

            def step(S, inp):
                qt, kt, vt, gt = inp
                S = jnp.exp(gt)[..., None] * S + kt[..., None] * vt[..., None, :]
                return (S, jnp.einsum('bhk,bhkv->bhv', qt, S))
            xs = tuple((jnp.moveaxis(a, 1, 0) for a in (q, k, v, gk)))
            S0 = jnp.zeros((q.shape[0], q.shape[2], q.shape[3], v.shape[3]), q.dtype)
            _, o = jax.lax.scan(step, S0, xs)
            return jnp.moveaxis(o, 0, 1)
        Bb, Tt, _ = x.shape
        h = _ln(x, ln_w, ln_b)
        q = (h @ Wq).reshape(Bb, Tt, HEADS, DK)
        k = (h @ Wk).reshape(Bb, Tt, HEADS, DK)
        v = (h @ Wv).reshape(Bb, Tt, HEADS, DV)
        gk = jax.nn.log_sigmoid(h @ gk_w1 @ gk_w2 + gk_b2) / GATE_NORM
        gk = gk.reshape(Bb, Tt, HEADS, DK)
        o = _gla(q * DK ** (-0.5), k, v, gk)
        g = (h @ Wg).reshape(Bb, Tt, HEADS, DV)
        o = _rms(o, rms_w) * (g * jax.nn.sigmoid(g))
        x = x + o.reshape(Bb, Tt, HEADS * DV) @ Wo
        h2 = _ln(x, ln_w, ln_b)
        return x + jax.nn.gelu(h2 @ W1 + b1, approximate=False) @ W2 + b2

    def _L0_ffn_ref(x, gate_w, gate_b, w1, b1, w2, b2):
        import jax, jax.numpy as jnp
        import numpy as np
        B, S, D, E, K = (4, 256, 128, 8, 2)
        H = 4 * D
        Bx, Sx, Dx = x.shape
        n_exp = w1.shape[0]
        logits = jnp.einsum('bsd,de->bse', x, gate_w) + gate_b
        scores = jax.nn.softmax(logits, axis=-1)
        topk_s, topk_i = jax.lax.top_k(scores, K)
        onehot = jax.nn.one_hot(topk_i, n_exp, dtype=scores.dtype)
        dispatch = jnp.einsum('bske,bsk->bse', onehot, topk_s)
        xf = x.reshape(-1, Dx)
        wf = dispatch.reshape(-1, n_exp)
        out = jnp.zeros_like(xf)
        for i in range(n_exp):
            wi = wf[:, i:i + 1]
            h = jax.nn.relu(xf * wi @ w1[i] + b1[i])
            y = h @ w2[i] + b2[i]
            out = jnp.where(wi > 0, y, out)
        return out.reshape(Bx, Sx, Dx)
    x = L0_attn_x
    x = _layernorm(x + _L0_attn_ref(x, L0_attn_ln_w, L0_attn_ln_b, L0_attn_Wq, L0_attn_Wk, L0_attn_Wv, L0_attn_gk_w1, L0_attn_gk_w2, L0_attn_gk_b2, L0_attn_Wg, L0_attn_rms_w, L0_attn_Wo, L0_attn_W1, L0_attn_b1, L0_attn_W2, L0_attn_b2), axis=-1)
    x = _layernorm(x + _L0_ffn_ref(x, L0_ffn_gate_w, L0_ffn_gate_b, L0_ffn_w1, L0_ffn_b1, L0_ffn_w2, L0_ffn_b2), axis=-1)
    return x

_drawn_inputs = setup_inputs


def setup_inputs(seed=0):
    import zlib

    import numpy as np

    out = dict(_drawn_inputs(seed))
    spreads = {'L0_attn_ln_w': (1.0, 0.6),
     'L0_attn_ln_b': (0.0, 0.551),
     'L0_attn_gk_b2': (0.0, 2.0),
     'L0_attn_rms_w': (1.0, 0.6),
     'L0_attn_b1': (0.0, 0.309),
     'L0_attn_b2': (0.0, 0.1),
     'L0_ffn_gate_b': (0.0, 0.1),
     'L0_ffn_b1': (0.0, 0.1),
     'L0_ffn_b2': (0.0, 0.1)}
    factors = {'L0_attn_gk_w1': 29.113, 'L0_attn_gk_w2': 24.491}
    for name, (base, spread) in spreads.items():
        noise = np.random.default_rng([zlib.crc32(name.encode()), seed]).standard_normal(out[name].shape)
        drawn = base * np.exp(spread * noise) if base else spread * noise
        out[name] = jnp.asarray(drawn.astype(out[name].dtype))
    for name, factor in factors.items():
        out[name] = (out[name] * factor).astype(out[name].dtype)
    return out
```

```python
from contextlib import ExitStack

import numpy as np

import concourse.bass as bass
from concourse import mybir

ALU = mybir.AluOpType
ACT = mybir.ActivationFunctionType
AX = mybir.AxisListType.X
F32 = mybir.dt.float32
BF16 = mybir.dt.bfloat16
I32 = mybir.dt.int32
U32 = mybir.dt.uint32

P = 128
D = 128
T = 256
B = 32
HEADS, DK, DV = 16, 4, 8
KD = HEADS * DK
LOW = 16
NTOK = B * T
NTILE = NTOK // P
PAIRS = B // 2
W4 = 4 * P
E, H = 8, 512
HC = H // P
FF = 2 * D
GT = 8
GROUPS = NTILE // GT
REC = D + 2
REGION = NTOK + P
SLOTS = NTILE + E - 1
NOWHERE = 1 << 20
EPS = 1e-5

VL = 4
C_ID, C_SEL = 0, P
C_UP = C_SEL + VL * P
C_REV = C_UP + P
C_J = C_REV + GT * E
C_BASE = C_J + SLOTS
C_128 = C_BASE + E
C_END = C_128 + NTILE


def constants():
    c = np.zeros((P, C_END), np.float32)
    r = np.arange(P)
    c[:, C_ID:C_ID + P] = np.eye(P)
    for v in range(VL):
        c[:, C_SEL + v * P:C_SEL + (v + 1) * P] = (r[:, None] // DK == r[None] // VL) & (r[None] % VL == v)
    c[:, C_UP:C_UP + P] = r[:, None] < r[None]
    c[:, C_REV:C_REV + GT * E] = np.tile(E - np.arange(E), GT)[None]
    c[:, C_J:C_J + SLOTS] = np.arange(SLOTS)[None]
    c[:, C_BASE:C_BASE + E] = REGION * np.arange(E)[None]
    c[:, C_128:C_128 + NTILE] = P * np.arange(NTILE)[None]
    return c


def token_numbers():
    return (np.arange(NTILE)[None] * P + np.arange(P)[:, None]).astype(np.int32)


class Chain:

    def __init__(self, sem, per_item):
        self.sem, self.per, self.n, self.item = sem, per_item, 0, 0

    def start(self, item):
        self.item, self.n = item, 0

    def link(self, ins):
        ins.then_inc(self.sem, 1)
        self.n += 1
        assert self.n <= self.per

    def join(self, eng):
        eng.wait_ge(self.sem, self.item * self.per + self.n)

    def end(self):
        assert self.n == self.per, (self.n, self.per)


def pipeline(eng, items, stages, first, unroll, step):
    assert (items - first) % unroll == 0 and first >= stages

    def written_out(k):
        step(k, k % unroll, lambda s: 0 <= k - s < items, lambda s: (k - s) // unroll)

    for k in range(first):
        written_out(k)
    with eng.Fori(0, (items - first) // unroll) as i:
        for u in range(unroll):
            step(i * unroll + (first + u), (first + u) % unroll, lambda s: True,
                 lambda s, u=u: i + (first + u - s) // unroll)
    for k in range(items, items + stages - 1):
        written_out(k)


def wait_items(eng, sem, item, back, per=1):
    if isinstance(item, int) and item - back + 1 <= 0:
        return
    eng.wait_ge(sem, (item - (back - 1)) * per)


def hold(eng):
    eng.nop(nofuse=True)


def gla_moe(nc, a, out):
    ctx = ExitStack()
    with ctx:
        def sb(name, shape, dt=F32):
            return ctx.enter_context(nc.sbuf_tensor(name, shape, dt))

        def carve(base, at, shape, dt=F32):
            n = int(np.prod(shape[1:]))
            view = base[:, at:at + n]
            names = "abcd"[:len(shape) - 1]
            view = view if dt == F32 else view.bitcast(dt)
            if len(shape) == 2:
                return view
            return view.rearrange(f"p ({' '.join(names)}) -> p {' '.join(names)}",
                                  **{c: m for c, m in zip(names, shape[1:])})

        def sem(name):
            return ctx.enter_context(nc.semaphore(name))

        bank = [ctx.enter_context(nc.psum_tensor(f"bank{i}", [P, 512], F32)) for i in range(8)]
        regions = nc.dram_tensor("expert_regions", (E * REGION + P, REC), F32, kind="Internal").ap()
        v_dram = nc.dram_tensor("values_by_head", (2, 2, HEADS, DV, T), F32, kind="Internal").ap()

        con = sb("con", [P, C_END])
        ident = con[:, C_ID:C_ID + P]
        sel_v = con[:, C_SEL:C_SEL + VL * P].rearrange("p (v c) -> p v c", v=VL)
        rev = con[:, C_REV:C_REV + GT * E].rearrange("p (g e) -> p g e", e=E)
        numbers = sb("numbers", [P, NTILE], I32)
        wq, wk = sb("wq", [P, KD]), sb("wk", [P, KD])
        wv, wg, wo, wo_raw = (sb(n, [P, D]) for n in ("wv", "wg", "wo", "wo_raw"))
        gk1, gk2, gk1t, wz = sb("gk1", [P, LOW]), sb("gk2", [LOW, KD]), sb("gk1t", [LOW, P]), sb("wz", [P, KD])
        w1, w2 = sb("w1", [P, FF]), sb("w2", [P, 2, D])
        b1 = sb("b1", [P, 2])
        b2 = sb("b2", [P, D])
        lnw, lnb, rmsw = sb("lnw", [P, 1]), sb("lnb", [P, 1]), sb("rmsw", [P, 1])
        gkb, gkb_neg = sb("gkb", [P, 1]), sb("gkb_neg", [P, 1])
        eps, one = sb("eps", [P, 1]), sb("one", [P, 1])
        gate_w, gate_b = sb("gate_w", [P, E]), sb("gate_b", [P, E])
        upper, ones = sb("upper", [P, P], BF16), sb("ones", [P, P], BF16)
        ew1, ew2 = sb("ew1", [P, E * H]), sb("ew2", [P, E * HC * D])
        eb1 = sb("eb1", [P, E * H])
        pad_record = sb("pad_record", [P, REC])

        x_sb = sb("x_sb", [P, NTILE * D])
        h2t = sb("h2t", [P, NTOK])

        st = sb("st", [P, 2, 4, 6])
        mv1, rs1, lv1 = sb("mv1", [P, 2, 4, 2]), sb("rs1", [P, 2, 4]), sb("lv1", [P, 4])
        st2, mv2, rs2, lv2 = sb("st2", [P, 4, 6]), sb("mv2", [P, 4, 2]), sb("rs2", [P, 4]), sb("lv2", [P, 4])
        row_buffers = sb("row_buffers", [P, 10 * W4])
        xn, vt, gate, og, xp = (carve(row_buffers, 2 * W4 * i, [P, 2, W4]) for i in range(5))
        ht = sb("ht", [P, W4])
        zg_abs, zg_neg = sb("zg_abs", [P, T + W4]), sb("zg_neg", [P, T + W4])
        decay, keys, queries = sb("decay", [P, 2, T]), sb("keys", [P, 2, T]), sb("queries", [P, 2, T])
        kv = sb("kv", [P, 2, DV * T])
        states = sb("states", [P, 2, DV * T])
        g_sig = sb("g_sig", [P, W4])
        o_rows, o_sq = sb("o_rows", [P, W4]), sb("o_sq", [P, W4])
        o_part, o_ss, o_lv = (sb(n, [P, P]) for n in ("o_part", "o_ss", "o_lv"))
        o_rs = sb("o_rs", [P, 2, P])
        ogt = sb("ogt", [P, W4])
        xn2 = sb("xn2", [P, W4])

        c_ld, w_ld, e_ld = sem("constants_loaded"), sem("weights_loaded"), sem("experts_loaded")
        setup_dve, setup_pe, eps_ready = sem("setup_dve"), sem("setup_pe"), sem("eps_ready")
        pad_ready, pad_out = sem("pad_record_ready"), sem("pad_block_written")
        SETUP = 4
        x_ld = sem("x_loaded")
        ln1_stats, ln1_rstd, ln1_norm = sem("ln1_stats"), sem("ln1_rstd"), sem("ln1_norm")
        t1_done, ht_done = sem("x_transposed"), sem("ht_ready")
        zk_done, v_done, q_done, g_done = (sem(n) for n in ("zk_done", "v_done", "q_done", "g_done"))
        z_parts, g_parts, zg_logged, zg_sum, decay_ready = (
            sem(n) for n in ("z_parts", "g_parts", "zg_logged", "zg_sum", "decay_ready"))
        v_sb, v_out, v_in = sem("v_evacuated"), sem("v_written"), sem("v_replicated")
        k_sb, q_sb = sem("k_evacuated"), sem("q_evacuated")
        g_sig_ready, gate_ready = sem("g_sig_ready"), sem("gate_ready")
        scanned, q_applied = sem("scanned"), sem("q_applied")
        o_done, o_evac, o_squared, o_summed, o_rstd = (sem(n) for n in ("o_done", "o_evac", "o_squared", "o_summed", "o_rstd"))
        o_gated, o_normed = sem("o_gated"), sem("o_normed")
        ogt_done, ogt_evac, y_done = sem("ogt_done"), sem("ogt_evac"), sem("y_done")
        xp_ready, ln2_stats, ln2_rstd, ln2_norm = (sem(n) for n in ("xp_ready", "ln2_stats", "ln2_rstd", "ln2_norm"))
        t2_done, h2t_done, x_summed = sem("t2_done"), sem("h2t_done"), sem("x_summed")
        dve_ln1 = Chain(sem("dve_ln1_chain"), 1)
        act_ln1 = Chain(sem("act_ln1_chain"), 1)
        act_z = Chain(sem("act_z_chain"), 2)
        dve_kv = Chain(sem("dve_kv_chain"), 1)
        dve_o = Chain(sem("dve_o_chain"), 1)
        act_o = Chain(sem("act_o_chain"), 1)
        dve_ln2 = Chain(sem("dve_ln2_chain"), 1)
        act_ln2 = Chain(sem("act_ln2_chain"), 1)

        STAGES_A, FIRST_A = 6, 6

        x_tok = a["x"].rearrange("(n g p) d -> p n g d", p=P, g=4)
        x_pairs = x_sb[:, :].rearrange("p (n g d) -> p n g d", g=4, d=D)


        def four(ap):
            return ap.rearrange("p (g d) -> p g d", g=4)

        eb2 = kv[:, :, :].rearrange("p a b -> p (a b)")[:, 3 * E * D:4 * E * D]

        def pair(ap, k):
            return ap[:, bass.ds(k, 1)].rearrange("p o g d -> p (o g) d")

        weight_loads = [(lnw[:, :], a["ln_w"]), (lnb[:, :], a["ln_b"]), (gk1[:, :], a["gk_w1"]), (gk2[:, :], a["gk_w2"]),
                        (gkb[0:KD, :], a["gk_b2"]), (gkb[KD:P, :], a["gk_b2"]), (wk[:, :], a["Wk"]), (wv[:, :], a["Wv"]),
                        (wq[:, :], a["Wq"]), (wg[:, :], a["Wg"]), (wo_raw[:, :], a["Wo"])]
        weight_loads += [(rmsw[VL * c:VL * c + VL, :], a["rms_w"][VL * (c // HEADS):VL * (c // HEADS) + VL, :])
                         for c in range(2 * HEADS)]

        weight_loads += [(numbers[:, :], a["numbers"]), (w1[:, :], a["W1"]), (w2[:, :, :], a["W2"].rearrange("(m p) d -> p m d", p=P)),
                         (b1[:, :], a["b1"]),
                         (b2[:, :], a["b2"].unsqueeze(0).to_broadcast([P, D])),
                         (gate_w[:, :], a["ffn_gate_w"]),
                         (gate_b[:, :], a["ffn_gate_b"].unsqueeze(0).to_broadcast([P, E]))]
        expert_loads = [(ew1[:, :].rearrange("p (e n) -> p e n", e=E), a["ffn_w1"].rearrange("e d n -> d e n")),
                        (ew2[:, :].rearrange("p (e c d) -> p (e c) d", e=E, c=HC),
                         a["ffn_w2"].rearrange("e (c p) d -> p (e c) d", p=P)),
                        (eb1[:, :], a["ffn_b1"].rearrange("e n -> (e n)").unsqueeze(0).to_broadcast([P, E * H])),
                        (eb2[:, :], a["ffn_b2"].rearrange("e n -> (e n)").unsqueeze(0).to_broadcast([P, E * D]))]
        STAGES_B, FIRST_B = 3, 4
        GW = GT * P
        u_t = kv[:, :, :].rearrange("p a b -> p (a b)")[:, 0:4 * 512].rearrange("p (h m n) -> p h m n", h=2, m=2)
        rows = states[:, :, :].rearrange("p a b -> p (a b)")[:, 0:2 * GW].rearrange("p (s n) -> p s n", s=2)
        x1t = states[:, :, :].rearrange("p a b -> p (a b)")[:, 2 * GW:3 * GW]
        rec = carve(row_buffers, 0, [P, 2, GT, REC])
        st3, mv3, lv3, rs3 = sb("st3", [P, GT, 6]), sb("mv3", [P, 2, GT, 2]), sb("lv3", [P, GT]), sb("rs3", [P, GT])
        logit, score, key, first_hot, tmp = (sb(n, [P, GT, E]) for n in ("logit", "score", "key", "first_hot", "tmp"))
        picked = sb("picked", [P, 2, GT, E], BF16)
        top, total, inv, top1, top2, rev1, rev2, gone, row_f = (
            sb(n, [P, GT]) for n in ("top", "total", "inv", "top1", "top2", "rev1", "rev2", "gone", "row_f"))
        row_i = sb("row_i", [P, 2, GT], I32)
        next_row = sb("next_row", [P, E])
        b_added, w1_done, gelu_done, w2_done, r_done = (sem(n) for n in ("b_added", "w1_done", "gelu_done", "w2_done", "r_done"))
        ln3_stats, ln3_rstd, ln3_norm = sem("ln3_stats"), sem("ln3_rstd"), sem("ln3_norm")
        t3_done, x1t_evac, logits_done = sem("t3_done"), sem("x1t_evac"), sem("logits_done")
        shifted, exped, picked_ready, prefix_done, rows_ready = (
            sem(n) for n in ("shifted", "exped", "picked_ready", "prefix_done", "rows_ready"))
        scattered = sem("scattered")
        dve_ln3, act_ln3 = Chain(sem("dve_ln3_chain"), 1), Chain(sem("act_ln3_chain"), 1)
        dve_shift = Chain(sem("dve_shift_chain"), 2)
        dve_pick = Chain(sem("dve_pick_chain"), 18)
        dve_row = Chain(sem("dve_row_chain"), 3)
        rec_i = rec[:, :, :, :].bitcast(I32)

        def over_experts(ap):
            return ap.unsqueeze(2).to_broadcast([P, GT, E])

        def phase_b_pe(pe):
            pe.wait_ge(h2t_done, PAIRS)
            pe.wait_ge(x_summed, PAIRS)

            def step(k, slot, live, turn):
                if live(0):
                    item = k
                    for hh in range(2):
                        for m in range(2):
                            if not (isinstance(item, int) and item == 0 and hh == 0):
                                pe.wait_ge(gelu_done, item * 4 + (2 * hh + m - 1))
                            pe.matmul(bank[m][:, :], w1[:, m * P:(m + 1) * P],
                                      h2t[:, bass.ds(item * GW + hh * 512, 512)],
                                      start=True, stop=True).then_inc(w1_done, 1)
                if live(0):
                    item = k
                    for hh in range(2):
                        pe.wait_ge(gelu_done, item * 4 + (2 * hh + 2))
                        if not (isinstance(item, int) and item == 0):
                            pe.wait_ge(r_done, item * 2 + (hh - 1))
                        for g in range(4):
                            for m in range(2):
                                ins = pe.matmul(bank[2 + hh][:, g * P:(g + 1) * P],
                                                u_t[:, hh, m, g * P:(g + 1) * P], w2[:, m, :],
                                                start=(m == 0), stop=(m == 1))
                        ins.then_inc(w2_done, 1)
                if live(2):
                    item, s = k - 2, slot % 2
                    pe.wait_ge(picked_ready, item + 1)
                    wait_items(pe, rows_ready, item, 1)
                    hot = picked[:, s, :, :].rearrange("p g e -> p (g e)")
                    pe.matmul(bank[7][:, 0:GT * E], upper[:, :], hot, start=True, stop=False)
                    for d in range(1, GT):
                        pe.matmul(bank[7][:, d * E:GT * E], ones[:, :], hot[:, 0:(GT - d) * E], start=False,
                                  stop=(d == GT - 1))
                    for g in range(GT):
                        ins = pe.matmul(bank[7][:, GT * E:GT * E + E], ones[:, :], hot[:, g * E:(g + 1) * E],
                                        start=(g == 0), stop=(g == GT - 1))
                    ins.then_inc(prefix_done, 1)
                if live(1):
                    item, s = k - 1, (slot - 1) % 2
                    pe.wait_ge(ln3_norm, item + 1)
                    wait_items(pe, x1t_evac, item, 1)
                    for g in range(GT):
                        ins = pe.transpose(bank[4 + g // 4][:, (g % 4) * P:(g % 4 + 1) * P], rec[:, s, g, 0:D], ident)
                    ins.then_inc(t3_done, 1)
                    pe.wait_ge(x1t_evac, item + 1)
                    wait_items(pe, shifted, item, 1)
                    for g in range(GT):
                        ins = pe.matmul(bank[6][:, g * E:(g + 1) * E], x1t[:, g * P:(g + 1) * P], gate_w[:, :],
                                        start=True, stop=True)
                    ins.then_inc(logits_done, 1)

            pipeline(pe, GROUPS, STAGES_B, FIRST_B, 2, step)

        def phase_b_act(act):
            act.wait_ge(x_summed, PAIRS)

            def step(k, slot, live, turn):
                act.preload_act_table_set("natural_log_exp_and_others")
                if live(1):
                    item, s = k - 1, (slot - 1) % 2
                    act.wait_ge(ln3_stats, item + 1)
                    act_ln3.start(item)
                    act_ln3.link(act.activation(lv3[:, :], mv3[:, s, :, 1], ACT.Ln, bias=eps[:, :]))
                    act_ln3.join(act)
                    act.activation(rs3[:, :], lv3[:, :], ACT.Exp, scale=-0.5).then_inc(ln3_rstd, 1)
                    act_ln3.end()
                if live(2):
                    act.wait_ge(shifted, (k - 2) + 1)
                    act.activation(score[:, :, :], logit[:, :, :], ACT.Exp).then_inc(exped, 1)
                if live(0):
                    item = k
                    for hh in range(2):
                        for m in range(2):
                            act.wait_ge(w1_done, item * 4 + (2 * hh + m + 1))
                            if not (isinstance(item, int) and item == 0):
                                act.wait_ge(w2_done, item * 2 + (hh - 1))
                            act.activation(u_t[:, hh, m, :], bank[m][:, :], ACT.Gelu,
                                           bias=b1[:, m:m + 1]).then_inc(gelu_done, 1)
                if live(1):
                    item = k - 1
                    act.wait_ge(t3_done, item + 1)
                    wait_items(act, logits_done, item, 1)
                    act.activation(x1t[:, 0:512], bank[4][:, :], ACT.Copy)
                    act.activation(x1t[:, 512:1024], bank[5][:, :], ACT.Copy).then_inc(x1t_evac, 1)

            pipeline(act, GROUPS, STAGES_B, FIRST_B, 2, step)

        def phase_b_dve(dve):
            dve.wait_ge(x_summed, PAIRS)
            dve.tensor_copy(next_row[:, :], con[:, C_BASE:C_BASE + E])

            def step(k, slot, live, turn):
                if live(2):
                    item = k - 2
                    dve_shift.start(item)
                    dve.wait_ge(logits_done, item + 1)
                    dve_shift.link(dve.tensor_tensor(logit[:, :, :], bank[6][:, 0:GT * E].rearrange("p (g e) -> p g e", e=E),
                                                     gate_b[:, :].unsqueeze(1).to_broadcast([P, GT, E]), ALU.add))
                    dve_shift.join(dve)
                    dve_shift.link(dve.tensor_reduce(top[:, :], logit[:, :, :], AX, ALU.max))
                    dve_shift.join(dve)
                    dve.tensor_tensor(logit[:, :, :], logit[:, :, :], over_experts(top[:, :]),
                                      ALU.subtract).then_inc(shifted, 1)
                    dve_shift.end()
                if live(0):
                    item, s = k, slot % 2
                    dve.wait_ge(b_added, item + 1)
                    for hh in range(2):
                        dve.wait_ge(w2_done, item * 2 + (hh + 1))
                        dve.tensor_tensor(rows[:, s, hh * 512:(hh + 1) * 512], bank[2 + hh][:, :],
                                          x_sb[:, bass.ds(item * GW + hh * 512, 512)], ALU.add).then_inc(r_done, 1)
                    dve.wait_ge(r_done, item * 2 + 2)
                    dve_ln3.start(item)
                    for g in range(GT):
                        ins = dve.bn_stats(st3[:, g, :], rows[:, s, g * P:(g + 1) * P])
                    dve_ln3.link(ins)
                    dve_ln3.join(dve)
                    hold(dve)
                    for g in range(GT):
                        ins = dve.bn_aggr(mv3[:, s, g, :], st3[:, g, :])
                    ins.then_inc(ln3_stats, 1)
                    dve_ln3.end()
                if live(2):
                    item, s = k - 2, slot % 2
                    c = dve_pick
                    c.start(item)

                    def then(ins):
                        c.link(ins)
                        c.join(dve)

                    dve.wait_ge(exped, item + 1)
                    then(dve.tensor_reduce(total[:, :], score[:, :, :], AX, ALU.add))
                    then(dve.reciprocal(inv[:, :], total[:, :]))
                    then(dve.tensor_tensor(score[:, :, :], score[:, :, :], over_experts(inv[:, :]), ALU.mult))
                    then(dve.tensor_reduce(top1[:, :], score[:, :, :], AX, ALU.max))
                    then(dve.tensor_tensor(key[:, :, :], score[:, :, :], over_experts(top1[:, :]), ALU.is_equal))
                    then(dve.tensor_tensor(key[:, :, :], key[:, :, :], rev, ALU.mult))
                    then(dve.tensor_reduce(rev1[:, :], key[:, :, :], AX, ALU.max))
                    then(dve.tensor_tensor(first_hot[:, :, :], rev, over_experts(rev1[:, :]), ALU.is_equal))
                    then(dve.scalar_tensor_tensor(tmp[:, :, :], first_hot[:, :, :], -2.0, score[:, :, :], ALU.mult, ALU.add))
                    then(dve.tensor_reduce(top2[:, :], tmp[:, :, :], AX, ALU.max))
                    then(dve.tensor_tensor(key[:, :, :], tmp[:, :, :], over_experts(top2[:, :]), ALU.is_equal))
                    then(dve.tensor_tensor(key[:, :, :], key[:, :, :], rev, ALU.mult))
                    then(dve.tensor_reduce(rev2[:, :], key[:, :, :], AX, ALU.max))
                    then(dve.tensor_scalar(gone[:, :], top2[:, :], 0.0, float(E), ALU.is_le, ALU.mult))
                    then(dve.tensor_tensor(rev2[:, :], rev2[:, :], gone[:, :], ALU.add))
                    then(dve.tensor_tensor(rev1[:, :], rev1[:, :], rev2[:, :], ALU.min))
                    dve.tensor_tensor(picked[:, s, :, :], rev, over_experts(rev1[:, :]), ALU.is_equal).then_inc(picked_ready, 1)
                    dve.wait_ge(picked_ready, item + 1)
                    then(dve.tensor_tensor(tmp[:, :, :], score[:, :, :], picked[:, s, :, :], ALU.mult))
                    then(dve.tensor_reduce(rec[:, s, :, D], tmp[:, :, :], AX, ALU.add))
                    hold(dve)
                    dve.tensor_copy(rec_i[:, s, :, D + 1], numbers[:, bass.ds(item * GT, GT)])
                    c.end()
                if live(1):
                    item, s = k - 1, (slot - 1) % 2
                    dve.wait_ge(ln3_rstd, item + 1)
                    wait_items(dve, scattered, item, 2, 16 * GT)
                    for g in range(GT):
                        ins = dve.tensor_scalar(rec[:, s, g, 0:D], rows[:, s, g * P:(g + 1) * P],
                                                mv3[:, s, g, 0:1], rs3[:, g:g + 1], ALU.subtract, ALU.mult)
                    ins.then_inc(ln3_norm, 1)
                if live(2):
                    item, s = k - 2, slot % 2
                    dve_row.start(item)
                    dve.wait_ge(prefix_done, item + 1)
                    dve_row.link(dve.tensor_tensor(tmp[:, :, :], bank[7][:, 0:GT * E].rearrange("p (g e) -> p g e", e=E),
                                                   next_row[:, :].unsqueeze(1).to_broadcast([P, GT, E]), ALU.add))
                    dve_row.join(dve)
                    dve_row.link(dve.tensor_tensor(tmp[:, :, :], tmp[:, :, :], picked[:, s, :, :], ALU.mult))
                    dve_row.join(dve)
                    dve.tensor_tensor(next_row[:, :], next_row[:, :], bank[7][:, GT * E:GT * E + E], ALU.add)
                    dve_row.link(dve.tensor_reduce(row_f[:, :], tmp[:, :, :], AX, ALU.add))
                    dve_row.join(dve)
                    dve.tensor_copy(row_i[:, s, :], row_f[:, :]).then_inc(rows_ready, 1)
                    dve_row.end()

            pipeline(dve, GROUPS, STAGES_B, FIRST_B, 2, step)

        def phase_b_pool(pool):
            def step(k, slot, live, turn):
                if live(0):
                    hold(pool)
                    xs = x_sb[:, bass.ds(k * GW, GW)].rearrange("p (g d) -> p g d", d=D)
                    pool.tensor_tensor(xs, xs, b2[:, :].unsqueeze(1).to_broadcast([P, GT, D]), ALU.add).then_inc(b_added, 1)
                if live(2):
                    item, s = k - 2, slot % 2
                    pool.wait_ge(rows_ready, item + 1)
                    hold(pool)
                    for g in range(GT):
                        pool.indirect_dma_start(
                            out=regions, out_offset=bass.IndirectOffsetOnAxis(ap=row_i[:, s, g:g + 1].bitcast(U32), axis=0),
                            in_=rec[:, s, g, :], in_offset=None).then_inc(scattered, 16)

            pipeline(pool, GROUPS, STAGES_B, FIRST_B, 2, step)

        STAGES_C, FIRST_C, UNROLL_C = 4, 7, 4
        tab_cnt, tab_n, tab_end, tab_start = (sb(n, [P, E]) for n in ("tab_cnt", "tab_n", "tab_end", "tab_start"))
        scratch = kv[:, :, :].rearrange("p a b -> p (a b)")
        tab_big = scratch[:, 0:E * NTILE]
        tab_ge = scratch[:, 512:512 + SLOTS * E]
        tab_mul = scratch[:, 1100:1100 + SLOTS * E]
        slot_e, slot_row, slot_start = (sb(n, [P, SLOTS]) for n in ("slot_e", "slot_row", "slot_start"))
        slot_ei, slot_rowi = sb("slot_ei", [P, SLOTS], I32), sb("slot_rowi", [P, SLOTS], I32)
        pad_col, pad_f = sb("pad_col", [P, 1]), sb("pad_f", [P, E])
        pad_i = sb("pad_i", [P, E], I32)
        pads_ready, table_ready, padded = sem("pads_ready"), sem("table_ready"), sem("padded")
        dve_tab = Chain(sem("dve_table_chain"), 15)
        at = [0]

        def over_x(shape):
            view = carve(x_sb, at[0], shape)
            at[0] += int(np.prod(shape[1:]))
            return view

        rc, xb = over_x([P, UNROLL_C, REC]), over_x([P, UNROLL_C, D])
        c_xw, c_xwt, c_z = (over_x([P, 2, D]) for _ in range(3))
        c_y = over_x([P, UNROLL_C, D])
        c_h, c_ht = over_x([P, 2, H]), over_x([P, 2, H])
        c_st, c_mv, c_lv, c_rs = over_x([P, 6]), over_x([P, 2]), over_x([P, 1]), over_x([P, 1])
        rc_ld, out_sc = ([sem(f"{n}{q}") for q in range(UNROLL_C)] for n in ("record_loaded", "rows_stored"))
        xw_done, xwt_done, xwt_evac, h_done, hb_done, xb_done = (
            sem(n) for n in ("xw_done", "xwt_done", "xwt_evac", "h_done", "hb_done", "xb_done"))
        htt_done, relu_done, y2_done, c_stats, c_rstd, yn_ready = (
            sem(n) for n in ("h_transposed", "relu_done", "y2_done", "c_stats", "c_rstd", "rows_normed"))
        dve_c = Chain(sem("dve_c_chain"), 2)
        act_c = Chain(sem("act_c_chain"), 1)

        def expert_of(eng, item):
            return eng.value_load(slot_ei[0:1, bass.ds(item, 1)], min_val=0, max_val=E - 1)

        def stored_before(eng, q, turn):
            if not (isinstance(turn, int) and turn <= 0):
                eng.wait_ge(out_sc[q], turn * 16)

        def phase_c_loads(sp):
            sp.wait_ge(table_ready, 1)
            sp.wait_ge(scattered, 16 * NTILE)
            sp.wait_ge(padded, 16 * E)
            sp.wait_ge(pad_out, 16)

            def step(k, slot, live, turn):
                if live(0):
                    stored_before(sp, slot, turn(0))
                    row = sp.value_load(slot_rowi[0:1, bass.ds(k, 1)], min_val=0, max_val=E * REGION)
                    sp.dma_start(rc[:, slot, :], regions[bass.ds(row, P), :]).then_inc(rc_ld[slot], 16)

            pipeline(sp, SLOTS, STAGES_C, FIRST_C, UNROLL_C, step)
            for q in range(UNROLL_C):
                sp.wait_ge(out_sc[q], 16 * len(range(q, SLOTS, UNROLL_C)))

        def phase_c_pe(pe):
            pe.wait_ge(table_ready, 1)
            pe.wait_ge(e_ld, 16 * 4)

            def step(k, slot, live, turn):
                if live(1):
                    item, s = k - 1, (slot - 1) % 2
                    pe.wait_ge(xw_done, item + 1)
                    wait_items(pe, xwt_evac, item, 2)
                    pe.transpose(bank[s][:, 0:P], c_xw[:, s, :], ident).then_inc(xwt_done, 1)
                if live(2):
                    item, s = k - 2, (slot - 2) % 2
                    pe.wait_ge(hb_done, item + 1)
                    wait_items(pe, relu_done, item, 2)
                    for c in range(HC):
                        ins = pe.transpose(bank[4 + s][:, c * P:(c + 1) * P], c_h[:, s, c * P:(c + 1) * P], ident)
                    ins.then_inc(htt_done, 1)
                if live(1):
                    item, s = k - 1, (slot - 1) % 2
                    e = expert_of(pe, item)
                    pe.wait_ge(xwt_evac, item + 1)
                    wait_items(pe, hb_done, item, 2)
                    pe.matmul(bank[2 + s][:, :], c_xwt[:, s, :], ew1[:, bass.ds(e * H, H)],
                              start=True, stop=True).then_inc(h_done, 1)
                if live(2):
                    item, s = k - 2, (slot - 2) % 2
                    e = expert_of(pe, item)
                    pe.wait_ge(relu_done, item + 1)
                    wait_items(pe, c_stats, item, 2)
                    for c in range(HC):
                        ins = pe.matmul(bank[6 + s][:, 0:D], c_ht[:, s, c * P:(c + 1) * P],
                                        ew2[:, bass.ds(e * (HC * D) + c * D, D)], start=(c == 0), stop=(c == HC - 1))
                    ins.then_inc(y2_done, 1)

            pipeline(pe, SLOTS, STAGES_C, FIRST_C, UNROLL_C, step)

        def phase_c_act(act):
            act.preload_act_table_set("natural_log_exp_and_others")

            def step(k, slot, live, turn):
                if live(1):
                    item, s, q = k - 1, (slot - 1) % 2, (slot - 1) % 4
                    act.wait_ge(rc_ld[q], turn(1) * 16 + 16)
                    wait_items(act, xwt_done, item, 2)
                    act.activation(c_xw[:, s, :], rc[:, q, 0:D], ACT.Copy, scale=rc[:, q, D:D + 1]).then_inc(xw_done, 1)
                    act.wait_ge(xwt_done, item + 1)
                    wait_items(act, h_done, item, 2)
                    act.activation(c_xwt[:, s, :], bank[s][:, 0:P], ACT.Copy).then_inc(xwt_evac, 1)
                if live(2):
                    item, s = k - 2, (slot - 2) % 2
                    act.wait_ge(htt_done, item + 1)
                    wait_items(act, y2_done, item, 2)
                    act.activation(c_ht[:, s, :], bank[4 + s][:, :], ACT.Relu).then_inc(relu_done, 1)
                if live(3):
                    item = k - 3
                    act.wait_ge(c_stats, item + 1)
                    act_c.start(item)
                    act_c.link(act.activation(c_lv[:, :], c_mv[:, 1:2], ACT.Ln, bias=eps[:, :]))
                    act_c.join(act)
                    act.activation(c_rs[:, :], c_lv[:, :], ACT.Exp, scale=-0.5).then_inc(c_rstd, 1)
                    act_c.end()

            pipeline(act, SLOTS, STAGES_C, FIRST_C, UNROLL_C, step)

        def phase_c_dve(dve):
            c = dve_tab
            c.start(0)

            def then(ins):
                c.link(ins)
                c.join(dve)

            then(dve.tensor_copy(pad_col[:, :], numbers[:, 0:1]))
            then(dve.tensor_scalar(pad_f[:, :], next_row[:, :], pad_col[:, :], None, ALU.add))
            dve.tensor_copy(pad_i[:, :], pad_f[:, :]).then_inc(pads_ready, 1)
            then(dve.tensor_tensor(tab_cnt[:, :], next_row[:, :], con[:, C_BASE:C_BASE + E], ALU.subtract))
            big = tab_big.rearrange("p (e j) -> p e j", e=E)
            then(dve.tensor_tensor(big, tab_cnt[:, :].unsqueeze(2).to_broadcast([P, E, NTILE]),
                                   con[:, C_128:C_128 + NTILE].unsqueeze(1).to_broadcast([P, E, NTILE]), ALU.is_gt))
            then(dve.tensor_reduce(tab_n[:, :], big, AX, ALU.add))
            then(dve.tensor_tensor_scan(tab_end[:, :], ones[:, 0:E], tab_n[:, :], 0.0, ALU.mult, ALU.add))
            ge = tab_ge.rearrange("p (j e) -> p j e", e=E)
            mul = tab_mul.rearrange("p (j e) -> p j e", e=E)
            j3 = con[:, C_J:C_J + SLOTS].unsqueeze(2).to_broadcast([P, SLOTS, E])
            then(dve.tensor_tensor(ge, j3, tab_end[:, :].unsqueeze(1).to_broadcast([P, SLOTS, E]), ALU.is_ge))
            then(dve.tensor_reduce(slot_e[:, :], ge, AX, ALU.add))
            then(dve.tensor_tensor(mul, ge, tab_n[:, :].unsqueeze(1).to_broadcast([P, SLOTS, E]), ALU.mult))
            then(dve.tensor_reduce(slot_start[:, :], mul, AX, ALU.add))
            then(dve.tensor_tensor(slot_start[:, :], con[:, C_J:C_J + SLOTS], slot_start[:, :], ALU.subtract))
            then(dve.tensor_scalar(slot_start[:, :], slot_start[:, :], float(P), None, ALU.mult))
            then(dve.scalar_tensor_tensor(slot_row[:, :], slot_e[:, :], float(REGION), slot_start[:, :], ALU.mult, ALU.add))
            then(dve.tensor_scalar(slot_row[:, :], slot_row[:, :], float(E * REGION), None, ALU.min))
            then(dve.tensor_scalar(slot_e[:, :], slot_e[:, :], float(E - 1), None, ALU.min))
            dve.tensor_copy(slot_ei[:, :], slot_e[:, :])
            dve.tensor_copy(slot_rowi[:, :], slot_row[:, :]).then_inc(table_ready, 1)
            c.end()
            dve.wait_ge(table_ready, 1)
            dve.wait_ge(e_ld, 16 * 4)

            def step(k, slot, live, turn):
                if live(3):
                    item, s, q = k - 3, (slot - 3) % 2, (slot - 3) % 4
                    dve_c.start(item)
                    dve.wait_ge(y2_done, item + 1)
                    dve.wait_ge(xb_done, item + 1)
                    dve_c.link(dve.tensor_tensor(c_z[:, s, :], bank[6 + s][:, 0:D], xb[:, q, :], ALU.add))
                    dve_c.join(dve)
                    dve_c.link(dve.bn_stats(c_st[:, :], c_z[:, s, :]))
                    dve_c.join(dve)
                    hold(dve)
                    dve.bn_aggr(c_mv[:, :], c_st[:, :]).then_inc(c_stats, 1)
                    dve_c.end()
                if live(1):
                    item, s = k - 1, (slot - 1) % 2
                    e = expert_of(dve, item)
                    dve.wait_ge(h_done, item + 1)
                    wait_items(dve, htt_done, item, 2)
                    dve.tensor_tensor(c_h[:, s, :], bank[2 + s][:, :], eb1[:, bass.ds(e * H, H)],
                                      ALU.add).then_inc(hb_done, 1)
                if live(3):
                    item, s, q = k - 3, (slot - 3) % 2, (slot - 3) % 4
                    dve.wait_ge(c_rstd, item + 1)
                    stored_before(dve, q, turn(3))
                    dve.tensor_scalar(c_y[:, q, :], c_z[:, s, :], c_mv[:, 0:1], c_rs[:, :],
                                      ALU.subtract, ALU.mult).then_inc(yn_ready, 1)

            pipeline(dve, SLOTS, STAGES_C, FIRST_C, UNROLL_C, step)

        def phase_c_pool(pool):
            pool.wait_ge(pads_ready, 1)
            for e in range(E):
                pool.indirect_dma_start(
                    out=regions, out_offset=bass.IndirectOffsetOnAxis(ap=pad_i[:, e:e + 1].bitcast(U32), axis=0),
                    in_=pad_record[:, :], in_offset=None).then_inc(padded, 16)
            pool.wait_ge(table_ready, 1)
            pool.wait_ge(e_ld, 16 * 4)

            def step(k, slot, live, turn):
                if live(1):
                    item, q = k - 1, (slot - 1) % 4
                    e = expert_of(pool, item)
                    pool.wait_ge(rc_ld[q], turn(1) * 16 + 16)
                    wait_items(pool, c_stats, item, 4)
                    hold(pool)
                    pool.tensor_tensor(xb[:, q, :], rc[:, q, 0:D], eb2[:, bass.ds(e * D, D)], ALU.add).then_inc(xb_done, 1)
                if live(3):
                    item, s, q = k - 3, (slot - 3) % 2, (slot - 3) % 4
                    pool.wait_ge(yn_ready, item + 1)
                    hold(pool)
                    pool.indirect_dma_start(
                        out=out, out_offset=bass.IndirectOffsetOnAxis(ap=rc[:, q, D + 1:REC].bitcast(U32), axis=0),
                        in_=c_y[:, q, :], in_offset=None, bounds_check=NTOK - 1, oob_is_err=False).then_inc(out_sc[q], 16)

            pipeline(pool, SLOTS, STAGES_C, FIRST_C, UNROLL_C, step)

        block = ctx.enter_context(nc.Block())

        @block.sync
        def _(sp):
            sp.dma_start(con[:, :], a["con"]).then_inc(c_ld, 16)
            sp.dma_start(x_pairs[:, 0], x_tok[:, 0]).then_inc(x_ld, 16)
            for dst, src in weight_loads:
                sp.dma_start(dst, src).then_inc(w_ld, 16)
            sp.wait_ge(pad_ready, 1)
            sp.dma_start(regions[E * REGION:E * REGION + P, :], pad_record[:, :]).then_inc(pad_out, 16)

            def step(k, slot, live, turn):
                if live(0):
                    if not (isinstance(k, int) and k == 0):
                        sp.dma_start(pair(x_pairs, k), pair(x_tok, k)).then_inc(x_ld, 16)
                if live(1):
                    item, s = k - 1, (slot - 1) % 2
                    wait_items(sp, v_in, item, 2, 16)
                    sp.wait_ge(v_sb, item + 1)
                    sp.dma_start(v_dram[s].rearrange("b h v t -> (h v) b t"),
                                 vt[:, s, :].rearrange("p (b t) -> p b t", b=2)).then_inc(v_out, 16)
                    sp.wait_ge(v_out, item * 16 + 16)
                    wait_items(sp, scanned, item, 2)
                    for b in range(2):
                        src = v_dram[s, b].rearrange("h v t -> h (v t)").unsqueeze(1).to_broadcast([HEADS, DK, DV * T])
                        sp.dma_start(kv[b * KD:(b + 1) * KD, s, :], src).then_inc(v_in, 16)

            pipeline(sp, PAIRS, STAGES_A, FIRST_A, 2, step)
            sp.wait_ge(scanned, PAIRS)
            for dst, src in expert_loads:
                sp.dma_start(dst, src).then_inc(e_ld, 16)
            phase_c_loads(sp)

        @block.tensor
        def _(pe):
            pe.wait_ge(c_ld, 16)
            pe.wait_ge(w_ld, 16 * len(weight_loads))
            pe.transpose(bank[1][0:LOW, 0:P], gk1[:, :], ident).then_inc(setup_pe, 1)
            pe.wait_ge(setup_dve, 1)
            pe.matmul(bank[2][:, 0:KD], gk1t[:, :], gk2[:, :], start=True, stop=True).then_inc(setup_pe, 1)
            pe.wait_ge(setup_dve, SETUP)

            def step(k, slot, live, turn):
                if live(1):
                    item, s = k - 1, (slot - 1) % 2
                    pe.wait_ge(ln1_norm, item + 1)
                    wait_items(pe, h2t_done, item, 5)
                    for g in range(4):
                        ins = pe.transpose(bank[0][:, g * P:(g + 1) * P], xn[:, s, g * P:(g + 1) * P], ident)
                    ins.then_inc(t1_done, 1)
                if live(3):
                    item, s = k - 3, (slot - 3) % 2
                    pe.wait_ge(q_applied, item + 1)
                    wait_items(pe, o_squared, item, 1)
                    for th in range(2):
                        for v in range(DV):
                            cols = bank[5][:, :].rearrange("p (t b w n) -> p t b w n", t=2, b=2, w=2)[:, th, :, v // VL, :]
                            ins = pe.matmul(cols, states[:, s, v * T + th * P:v * T + th * P + P],
                                            sel_v[:, v % VL, :].rearrange("p (b n) -> p b n", b=2),
                                            start=(v % VL == 0), stop=(v % VL == VL - 1))
                    ins.then_inc(o_done, 1)
                if live(1):
                    item, s = k - 1, (slot - 1) % 2
                    pe.wait_ge(ht_done, item + 1)
                    wait_items(pe, v_sb, item, 1)
                    pe.matmul(bank[3][:, :], wv[:, :], ht[:, :], start=True, stop=True).then_inc(v_done, 1)
                    wait_items(pe, z_parts, item, 1)
                    wait_items(pe, k_sb, item, 1)
                    for col, w in ((0, wz), (T, wk)):
                        for b in range(2):
                            ins = pe.matmul(bank[1][b * KD:(b + 1) * KD, col:col + T], w[:, :],
                                            ht[:, b * T:(b + 1) * T], start=True, stop=True)
                    ins.then_inc(zk_done, 1)
                    wait_items(pe, q_sb, item, 1)
                    for b in range(2):
                        ins = pe.matmul(bank[2][b * KD:(b + 1) * KD, 0:T], wq[:, :], ht[:, b * T:(b + 1) * T],
                                        start=True, stop=True)
                    ins.then_inc(q_done, 1)
                    wait_items(pe, gate_ready, item, 1)
                    for th in range(2):
                        for b in range(2):
                            col, tok = (2 * th + b) * P, b * T + th * P
                            ins = pe.matmul(bank[4][:, col:col + P], ht[:, tok:tok + P], wg[:, :],
                                            start=True, stop=True)
                    ins.then_inc(g_done, 1)
                if live(4):
                    item, s = k - 4, (slot - 4) % 2
                    pe.wait_ge(o_normed, item + 1)
                    wait_items(pe, ogt_evac, item, 1)
                    for th in range(2):
                        for b in range(2):
                            col, tok = (2 * th + b) * P, b * T + th * P
                            ins = pe.transpose(bank[6][:, tok:tok + P], og[:, s, col:col + P], ident)
                    ins.then_inc(ogt_done, 1)
                if live(5):
                    item = k - 5
                    pe.wait_ge(ln2_norm, item + 1)
                    if live(1):
                        pe.wait_ge(ht_done, item + 5)
                    else:
                        pe.wait_ge(h2t_done, item)
                    for g in range(4):
                        ins = pe.transpose(bank[0][:, g * P:(g + 1) * P], xn2[:, g * P:(g + 1) * P], ident)
                    ins.then_inc(t2_done, 1)
                if live(4):
                    item = k - 4
                    pe.wait_ge(ogt_evac, item + 1)
                    wait_items(pe, xp_ready, item, 1)
                    for g in range(4):
                        ins = pe.matmul(bank[7][:, g * P:(g + 1) * P], ogt[:, g * P:(g + 1) * P], wo[:, :],
                                        start=True, stop=True)
                    ins.then_inc(y_done, 1)

            pipeline(pe, PAIRS, STAGES_A, FIRST_A, 2, step)
            phase_b_pe(pe)
            phase_c_pe(pe)

        @block.scalar
        def _(act):
            act.preload_act_table_set("natural_log_exp_and_others")
            act.wait_ge(eps_ready, 2)
            act.wait_ge(w_ld, 16 * len(weight_loads))
            act.wait_ge(setup_dve, SETUP)

            def step(k, slot, live, turn):
                if live(2):
                    item, s = k - 2, slot % 2
                    act.wait_ge(zg_sum, item + 1)
                    act.activation(decay[:, s, :], zg_neg[:, 0:T], ACT.Exp, scale=-1.0 / 16).then_inc(decay_ready, 1)
                    wait_items(act, gate_ready, item, 1)
                    act.activation(g_sig[:, :], zg_neg[:, T:], ACT.Exp, scale=-1.0).then_inc(g_sig_ready, 1)
                if live(5):
                    item = k - 5
                    act.wait_ge(ln2_stats, item + 1)
                    act_ln2.start(item)
                    act_ln2.link(act.activation(lv2[:, :], mv2[:, :, 1], ACT.Ln, bias=eps[:, :]))
                    act_ln2.join(act)
                    act.activation(rs2[:, :], lv2[:, :], ACT.Exp, scale=-0.5).then_inc(ln2_rstd, 1)
                    act_ln2.end()
                if live(1):
                    item = k - 1
                    act.wait_ge(t1_done, item + 1)
                    wait_items(act, g_done, item, 1)
                    act.activation(ht[:, :], bank[0][:, :], ACT.Identity, bias=lnb[:, :],
                                   scale=lnw[:, :]).then_inc(ht_done, 1)
                if live(3):
                    item = k - 3
                    act.wait_ge(o_done, item + 1)
                    wait_items(act, o_gated, item, 1)
                    act.activation(o_rows[:, :], bank[5][:, :], ACT.Copy).then_inc(o_evac, 1)
                    wait_items(act, o_summed, item, 1)
                    act.activation(o_sq[:, :], bank[5][:, :], ACT.Square).then_inc(o_squared, 1)
                if live(1):
                    item, s = k - 1, (slot - 1) % 2
                    act.wait_ge(v_done, item + 1)
                    wait_items(act, v_out, item, 2, 16)
                    act.activation(vt[:, s, :], bank[3][:, :], ACT.Copy).then_inc(v_sb, 1)
                    act.wait_ge(zk_done, item + 1)
                    wait_items(act, zg_sum, item, 1)
                    act.activation(zg_abs[:, 0:T], bank[1][:, 0:T], ACT.Abs, bias=gkb[:, :])
                    act.activation(zg_neg[:, 0:T], bank[1][:, 0:T], ACT.Relu, bias=gkb_neg[:, :],
                                   scale=-1.0).then_inc(z_parts, 1)
                    wait_items(act, scanned, item, 2)
                    act.activation(keys[:, s, :], bank[1][:, T:2 * T], ACT.Copy).then_inc(k_sb, 1)
                    act.wait_ge(g_done, item + 1)
                    act_z.start(item)
                    act.activation(zg_neg[:, T:], bank[4][:, :], ACT.Relu, scale=-1.0)
                    act_z.link(act.activation(zg_abs[:, T:], bank[4][:, :], ACT.Abs))
                    act_z.join(act)
                    act_z.link(act.activation(zg_abs[:, :], zg_abs[:, :], ACT.Exp, scale=-1.0))
                    act_z.join(act)
                    act.activation(zg_abs[:, :], zg_abs[:, :], ACT.Ln, bias=one[:, :]).then_inc(zg_logged, 1)
                    act_z.end()
                    act.wait_ge(q_done, item + 1)
                    wait_items(act, q_applied, item, 2)
                    act.activation(queries[:, s, :], bank[2][:, 0:T], ACT.Copy, scale=DK ** -0.5).then_inc(q_sb, 1)
                if live(3):
                    item, s = k - 3, (slot - 3) % 2
                    act.wait_ge(o_summed, item + 1)
                    act_o.start(item)
                    act_o.link(act.activation(o_lv[:, :], o_ss[:, :], ACT.Ln, bias=eps[:, :], scale=1.0 / DV))
                    act_o.join(act)
                    wait_items(act, o_normed, item, 2)
                    act.activation(o_rs[:, s, :], o_lv[:, :], ACT.Exp, scale=-0.5).then_inc(o_rstd, 1)
                    act_o.end()
                if live(0):
                    item, s = k, slot % 2
                    act.wait_ge(ln1_stats, item + 1)
                    act_ln1.start(item)
                    act_ln1.link(act.activation(lv1[:, :], mv1[:, s, :, 1], ACT.Ln, bias=eps[:, :]))
                    act_ln1.join(act)
                    act.activation(rs1[:, s, :], lv1[:, :], ACT.Exp, scale=-0.5).then_inc(ln1_rstd, 1)
                    act_ln1.end()
                if live(4):
                    item = k - 4
                    act.wait_ge(ogt_done, item + 1)
                    wait_items(act, y_done, item, 1)
                    act.activation(ogt[:, :], bank[6][:, :], ACT.Copy).then_inc(ogt_evac, 1)
                if live(5):
                    item = k - 5
                    act.wait_ge(t2_done, item + 1)
                    hold(act)
                    act.activation(h2t[:, bass.ds(item * W4, W4)], bank[0][:, :], ACT.Identity, bias=lnb[:, :],
                                   scale=lnw[:, :]).then_inc(h2t_done, 1)

            pipeline(act, PAIRS, STAGES_A, FIRST_A, 2, step)
            phase_b_act(act)
            phase_c_act(act)

        @block.vector
        def _(dve):
            dve.memset(eps[:, :], EPS).then_inc(eps_ready, 1)
            dve.memset(one[:, :], 1.0).then_inc(eps_ready, 1)
            dve.memset(pad_record[:, 0:D + 1], 0.0)
            dve.memset(pad_record[:, D + 1:REC].bitcast(I32), NOWHERE).then_inc(pad_ready, 1)
            dve.wait_ge(c_ld, 16)
            dve.wait_ge(w_ld, 16 * len(weight_loads))
            dve.wait_ge(setup_pe, 1)
            dve.tensor_copy(gk1t[:, :], bank[1][0:LOW, 0:P]).then_inc(setup_dve, 1)
            dve.tensor_copy(upper[:, :], con[:, C_UP:C_UP + P])
            dve.memset(ones[:, :], 1.0)
            dve.tensor_scalar(wo[:, :], wo_raw[:, :], rmsw[:, :], None, ALU.mult).then_inc(setup_dve, 1)
            dve.tensor_scalar(gkb_neg[:, :], gkb[:, :], -1.0, None, ALU.mult).then_inc(setup_dve, 1)
            dve.wait_ge(setup_pe, 2)
            dve.tensor_copy(wz[:, :], bank[2][:, 0:KD]).then_inc(setup_dve, 1)

            def step(k, slot, live, turn):
                if live(5):
                    item, s = k - 5, (slot - 5) % 2
                    dve.wait_ge(y_done, item + 1)
                    wait_items(dve, x_summed, item, 2)
                    dve.tensor_tensor(xp[:, s, :], bank[7][:, :], x_sb[:, bass.ds(item * W4, W4)],
                                      ALU.add).then_inc(xp_ready, 1)
                    dve.wait_ge(xp_ready, item + 1)
                    dve_ln2.start(item)
                    for g in range(4):
                        ins = dve.bn_stats(st2[:, g, :], xp[:, s, g * P:(g + 1) * P])
                    dve_ln2.link(ins)
                    dve_ln2.join(dve)
                    hold(dve)
                    for g in range(4):
                        ins = dve.bn_aggr(mv2[:, g, :], st2[:, g, :])
                    ins.then_inc(ln2_stats, 1)
                    dve_ln2.end()
                if live(2):
                    item, s = k - 2, (slot - 2) % 2
                    dve.wait_ge(v_in, item * 32 + 32)
                    dve.wait_ge(k_sb, item + 1)
                    dve_kv.start(item)
                    kv3 = kv[:, s, :].rearrange("p (v t) -> p v t", v=DV)
                    dve_kv.link(dve.tensor_tensor(kv3, kv3, keys[:, s, :].unsqueeze(1).to_broadcast([P, DV, T]),
                                                  ALU.mult))
                    dve_kv.join(dve)
                    dve.wait_ge(decay_ready, item + 1)
                    wait_items(dve, o_done, item, 2)
                    for v in range(DV):
                        ins = dve.tensor_tensor_scan(states[:, s, v * T:(v + 1) * T], decay[:, s, :],
                                                     kv[:, s, v * T:(v + 1) * T], 0.0, ALU.mult, ALU.add)
                    ins.then_inc(scanned, 1)
                    dve_kv.end()
                if live(2):
                    item, s = k - 2, slot % 2
                    dve.wait_ge(g_sig_ready, item + 1)
                    wait_items(dve, o_gated, item, 2)
                    dve.tensor_tensor(gate[:, s, :], bank[4][:, :], g_sig[:, :], ALU.mult).then_inc(gate_ready, 1)
                if live(0):
                    item, s = k, slot % 2
                    dve.wait_ge(x_ld, item * 16 + 16)
                    hold(dve)
                    dve_ln1.start(item)
                    for g in range(4):
                        ins = dve.bn_stats(st[:, s, g, :], x_sb[:, bass.ds(item * W4 + g * P, P)])
                    dve_ln1.link(ins)
                    dve_ln1.join(dve)
                    hold(dve)
                    for g in range(4):
                        ins = dve.bn_aggr(mv1[:, s, g, :], st[:, s, g, :])
                    ins.then_inc(ln1_stats, 1)
                    dve_ln1.end()
                if live(5):
                    item, s = k - 5, (slot - 5) % 2
                    dve.wait_ge(ln2_rstd, item + 1)
                    wait_items(dve, t2_done, item, 1)
                    for g in range(4):
                        ins = dve.tensor_scalar(xn2[:, g * P:(g + 1) * P], xp[:, s, g * P:(g + 1) * P],
                                                mv2[:, g, 0:1], rs2[:, g:g + 1], ALU.subtract, ALU.mult)
                    ins.then_inc(ln2_norm, 1)
                if live(3):
                    item = k - 3
                    dve.wait_ge(o_squared, item + 1)
                    wait_items(dve, o_rstd, item, 1)
                    dve_o.start(item)
                    dve_o.link(dve.tensor_reduce(o_part[:, :], o_sq[:, :].rearrange("p (c v) -> p c v", v=VL), AX,
                                                 ALU.add))
                    dve_o.join(dve)
                    part = o_part[:, :].rearrange("p (t w c) -> p t w c", t=4, w=2)
                    whole = o_ss[:, :].rearrange("p (t w c) -> p t w c", t=4, w=2)
                    for w in range(2):
                        ins = dve.tensor_tensor(whole[:, :, w, :], part[:, :, 0, :], part[:, :, 1, :], ALU.add)
                    ins.then_inc(o_summed, 1)
                    dve_o.end()
                if live(0):
                    item, s = k, slot % 2
                    dve.wait_ge(ln1_rstd, item + 1)
                    wait_items(dve, t1_done, item, 2)
                    for g in range(4):
                        ins = dve.tensor_scalar(xn[:, s, g * P:(g + 1) * P], x_sb[:, bass.ds(item * W4 + g * P, P)],
                                                mv1[:, s, g, 0:1], rs1[:, s, g:g + 1], ALU.subtract, ALU.mult)
                    ins.then_inc(ln1_norm, 1)

            pipeline(dve, PAIRS, STAGES_A, FIRST_A, 2, step)
            phase_b_dve(dve)
            phase_c_dve(dve)

        @block.gpsimd
        def _(pool):
            def step(k, slot, live, turn):
                if live(4):
                    item, s = k - 4, (slot - 4) % 2
                    pool.wait_ge(o_rstd, item + 1)
                    pool.wait_ge(o_gated, item + 1)
                    hold(pool)
                    og3 = og[:, s, :].rearrange("p (c v) -> p c v", v=VL)
                    pool.tensor_tensor(og3, og3, o_rs[:, s, :].unsqueeze(2).to_broadcast([P, P, VL]),
                                       ALU.mult).then_inc(o_normed, 1)
                if live(5):
                    item, s = k - 5, (slot - 5) % 2
                    pool.wait_ge(xp_ready, item + 1)
                    hold(pool)
                    xs = x_sb[:, bass.ds(item * W4, W4)]
                    pool.tensor_tensor(xs, xs, xp[:, s, :], ALU.add).then_inc(x_summed, 1)
                if live(3):
                    item, s = k - 3, (slot - 3) % 2
                    pool.wait_ge(o_evac, item + 1)
                    pool.wait_ge(gate_ready, item + 1)
                    wait_items(pool, ogt_done, item, 2)
                    hold(pool)
                    pool.tensor_tensor(og[:, s, :], o_rows[:, :], gate[:, s, :], ALU.mult).then_inc(o_gated, 1)
                if live(2):
                    item, s = k - 2, (slot - 2) % 2
                    pool.wait_ge(q_sb, item + 1)
                    pool.wait_ge(scanned, item + 1)
                    hold(pool)
                    st3 = states[:, s, :].rearrange("p (v t) -> p v t", v=DV)
                    pool.tensor_tensor(st3, st3, queries[:, s, :].unsqueeze(1).to_broadcast([P, DV, T]),
                                       ALU.mult).then_inc(q_applied, 1)
                if live(1):
                    item = k - 1
                    pool.wait_ge(z_parts, item + 1)
                    pool.wait_ge(zg_logged, item + 1)
                    hold(pool)
                    pool.tensor_tensor(zg_neg[:, :], zg_neg[:, :], zg_abs[:, :], ALU.add).then_inc(zg_sum, 1)

            pipeline(pool, PAIRS, STAGES_A, FIRST_A, 2, step)
            phase_b_pool(pool)
            phase_c_pool(pool)


def kernel(**inputs):
    import numpy as _np
    import concourse.bacc as _bacc
    from concourse import mybir as _mybir
    from concourse.bass_utils import run_bass_kernel_spmd as _run

    arrays = {"con": constants(), "numbers": token_numbers()}
    for name, value in inputs.items():
        v = _np.ascontiguousarray(value)
        key = name.replace("L0_attn_", "").replace("L0_ffn_", "ffn_")
        if key == "x":
            v = v.reshape(NTOK, D)
        elif key in ("ln_w", "ln_b", "gk_b2", "rms_w"):
            v = v.reshape(-1, 1)
        elif key == "Wg":
            v = _np.ascontiguousarray(v.reshape(D, HEADS, 2, VL).transpose(0, 2, 1, 3)).reshape(D, D)
        elif key == "Wo":
            v = _np.ascontiguousarray(v.reshape(HEADS, 2, VL, D).transpose(1, 0, 2, 3)).reshape(D, D)
        elif key == "b1":
            v = _np.ascontiguousarray(v.reshape(2, P).T)
        arrays[key] = v
    nc = _bacc.Bacc("TRN2", target_bir_lowering=False, num_devices=1)
    aps = {n: nc.dram_tensor(f"in_{n}", v.shape, _mybir.dt.from_np(v.dtype), kind="ExternalInput").ap()
           for n, v in arrays.items()}
    out = nc.dram_tensor("out_rows", (NTOK, D), _mybir.dt.float32, kind="ExternalOutput").ap()
    gla_moe(nc, aps, out)
    r = _run(nc, [{f"in_{n}": v for n, v in arrays.items()}], core_ids=[0])
    return r.results[0]["out_rows"].reshape(B, T, D)
```

```python
from contextlib import ExitStack

import numpy as np

import concourse.bass as bass
from concourse import mybir

ALU = mybir.AluOpType
ACT = mybir.ActivationFunctionType
AX = mybir.AxisListType.X
F32 = mybir.dt.float32
BF16 = mybir.dt.bfloat16
I32 = mybir.dt.int32
U32 = mybir.dt.uint32

P = 128
D = 128
T = 256
B = 32
HEADS, DK, DV = 16, 4, 8
KD = HEADS * DK
LOW = 16
NTOK = B * T
NTILE = NTOK // P
PAIRS = B // 2
W4 = 4 * P
E, H = 8, 512
HC = H // P
FF = 2 * D
GT = 8
GROUPS = NTILE // GT
REC = D + 2
REGION = NTOK + P
SLOTS = NTILE + E - 1
NOWHERE = 1 << 20
EPS = 1e-5

VL = 4
C_ID, C_SEL = 0, P
C_UP = C_SEL + VL * P
C_REV = C_UP + P
C_J = C_REV + GT * E
C_BASE = C_J + SLOTS
C_128 = C_BASE + E
C_END = C_128 + NTILE


PACKED = {"ln_w": 1, "ln_b": 1, "rms_w": 1, "gk_b2": 1, "gk_w1": LOW, "Wk": KD, "Wv": D, "Wq": KD, "Wg": D, "Wo": D}


def constants():
    c = np.zeros((P, C_END), np.float32)
    r = np.arange(P)
    c[:, C_ID:C_ID + P] = np.eye(P)
    for v in range(VL):
        c[:, C_SEL + v * P:C_SEL + (v + 1) * P] = (r[:, None] // DK == r[None] // VL) & (r[None] % VL == v)
    c[:, C_UP:C_UP + P] = r[:, None] < r[None]
    c[:, C_REV:C_REV + GT * E] = np.tile(E - np.arange(E), GT)[None]
    c[:, C_J:C_J + SLOTS] = np.arange(SLOTS)[None]
    c[:, C_BASE:C_BASE + E] = REGION * np.arange(E)[None]
    c[:, C_128:C_128 + NTILE] = P * np.arange(NTILE)[None]
    return c


def token_numbers():
    return (np.arange(NTILE)[None] * P + np.arange(P)[:, None]).astype(np.int32)


class Chain:

    def __init__(self, sem, per_item):
        self.sem, self.per, self.n, self.item = sem, per_item, 0, 0

    def start(self, item):
        self.item, self.n = item, 0

    def link(self, ins):
        ins.then_inc(self.sem, 1)
        self.n += 1
        assert self.n <= self.per

    def join(self, eng):
        eng.wait_ge(self.sem, self.item * self.per + self.n)

    def end(self):
        assert self.n == self.per, (self.n, self.per)


def pipeline(eng, items, stages, first, unroll, step, slots=None, before=None, after=None):
    slots = slots or unroll
    assert (items - first) % unroll == 0 and first >= stages and unroll % slots == 0

    def written_out(k):
        step(k, k % unroll, lambda s: 0 <= k - s < items, lambda s: (k - s) // slots)

    for k in range(first):
        written_out(k)
    if items > first:
        with eng.Fori(0, (items - first) // unroll) as i:
            for u in range(unroll):
                step(i * unroll + (first + u), (first + u) % unroll, lambda s: True,
                     lambda s, u=u: i * (unroll // slots) + (first + u - s) // slots)
    for k in range(items, items + stages - 1):
        if before:
            before(k)
        written_out(k)
        if after:
            after(k)


def wait_items(eng, sem, item, back, per=1):
    if isinstance(item, int) and item - back + 1 <= 0:
        return
    eng.wait_ge(sem, (item - (back - 1)) * per)


def hold(eng):
    eng.nop(nofuse=True)


def gla_moe(nc, a, out):
    ctx = ExitStack()
    with ctx:
        def sb(name, shape, dt=F32):
            return ctx.enter_context(nc.sbuf_tensor(name, shape, dt))

        def carve(base, at, shape, dt=F32):
            n = int(np.prod(shape[1:]))
            view = base[:, at:at + n]
            names = "abcd"[:len(shape) - 1]
            view = view if dt == F32 else view.bitcast(dt)
            if len(shape) == 2:
                return view
            return view.rearrange(f"p ({' '.join(names)}) -> p {' '.join(names)}",
                                  **{c: m for c, m in zip(names, shape[1:])})

        def sem(name):
            return ctx.enter_context(nc.semaphore(name))

        bank = [ctx.enter_context(nc.psum_tensor(f"bank{i}", [P, 512], F32)) for i in range(8)]
        regions = nc.dram_tensor("expert_regions", (E * REGION + P, REC), F32, kind="Internal").ap()
        v_dram = nc.dram_tensor("values_by_head", (2, 2, HEADS, DV, T), F32, kind="Internal").ap()

        con = sb("con", [P, C_END])
        ident = con[:, C_ID:C_ID + P]
        sel_v = con[:, C_SEL:C_SEL + VL * P].rearrange("p (v c) -> p v c", v=VL)
        rev = con[:, C_REV:C_REV + GT * E].rearrange("p (g e) -> p g e", e=E)
        numbers = sb("numbers", [P, NTILE], I32)
        packed = sb("packed", [P, sum(PACKED.values())])
        starts = np.cumsum([0] + list(PACKED.values())).tolist()
        field = {n: packed[:, at:at + w] for (n, w), at in zip(PACKED.items(), starts)}
        wk, wv, wq, wg, wo_raw, gk1 = (field[n] for n in ("Wk", "Wv", "Wq", "Wg", "Wo", "gk_w1"))
        lnw, lnb, rmsw, gkb = (field[n] for n in ("ln_w", "ln_b", "rms_w", "gk_b2"))
        wo, wz = sb("wo", [P, D]), sb("wz", [P, KD])
        gk2, gk1t = sb("gk2", [LOW, KD]), sb("gk1t", [LOW, P])
        w1, w2 = sb("w1", [P, FF]), sb("w2", [P, 2, D])
        b1 = sb("b1", [P, 2])
        b2 = sb("b2", [P, D])
        gkb_neg = sb("gkb_neg", [P, 1])
        eps, one = sb("eps", [P, 1]), sb("one", [P, 1])
        gate_w, gate_b = sb("gate_w", [P, E]), sb("gate_b", [P, E])
        upper, ones = sb("upper", [P, P], BF16), sb("ones", [P, P], BF16)
        ew1, ew2 = sb("ew1", [P, E * H]), sb("ew2", [P, E * HC * D])
        eb1 = sb("eb1", [P, E * H])
        pad_record = sb("pad_record", [P, REC])

        x_sb = sb("x_sb", [P, NTILE * D])
        h2t = sb("h2t", [P, NTOK])

        st = sb("st", [P, 2, 4, 6])
        mv1, rs1, lv1 = sb("mv1", [P, 2, 4, 2]), sb("rs1", [P, 2, 4]), sb("lv1", [P, 4])
        st2, mv2, rs2, lv2 = sb("st2", [P, 4, 6]), sb("mv2", [P, 4, 2]), sb("rs2", [P, 4]), sb("lv2", [P, 4])
        row_buffers = sb("row_buffers", [P, 10 * W4])
        xn, vt, gate, og, xp = (carve(row_buffers, 2 * W4 * i, [P, 2, W4]) for i in range(5))
        ht = sb("ht", [P, W4])
        zg_abs, zg_neg = sb("zg_abs", [P, T + W4]), sb("zg_neg", [P, T + W4])
        decay, keys, queries = sb("decay", [P, 2, T]), sb("keys", [P, 2, T]), sb("queries", [P, 2, T])
        kv = sb("kv", [P, 2, DV * T])
        states = sb("states", [P, 2, DV * T])
        g_sig = sb("g_sig", [P, W4])
        o_rows, o_sq = sb("o_rows", [P, W4]), sb("o_sq", [P, W4])
        o_part, o_ss, o_lv = (sb(n, [P, P]) for n in ("o_part", "o_ss", "o_lv"))
        o_rs = sb("o_rs", [P, 2, P])
        ogt = sb("ogt", [P, W4])
        xn2 = sb("xn2", [P, W4])

        w_ld, late_ld, e_ld = sem("weights_loaded"), sem("late_weights_loaded"), sem("experts_loaded")
        setup_dve, setup_pe, eps_ready = sem("setup_dve"), sem("setup_pe"), sem("eps_ready")
        pad_ready, pad_out = sem("pad_record_ready"), sem("pad_block_written")
        SETUP = 4
        x_ld = sem("x_loaded")
        ln1_stats, ln1_rstd, ln1_norm = sem("ln1_stats"), sem("ln1_rstd"), sem("ln1_norm")
        t1_done, ht_done = sem("x_transposed"), sem("ht_ready")
        zk_done, v_done, q_done, g_done = (sem(n) for n in ("zk_done", "v_done", "q_done", "g_done"))
        z_parts, g_parts, zg_logged, zg_sum, decay_ready = (
            sem(n) for n in ("z_parts", "g_parts", "zg_logged", "zg_sum", "decay_ready"))
        v_sb, v_out, v_in = sem("v_evacuated"), sem("v_written"), sem("v_replicated")
        k_sb, q_sb = sem("k_evacuated"), sem("q_evacuated")
        g_sig_ready, gate_ready = sem("g_sig_ready"), sem("gate_ready")
        scanned, q_applied = sem("scanned"), sem("q_applied")
        o_done, o_evac, o_squared, o_summed, o_rstd = (sem(n) for n in ("o_done", "o_evac", "o_squared", "o_summed", "o_rstd"))
        o_gated, o_normed = sem("o_gated"), sem("o_normed")
        ogt_done, ogt_evac, y_done = sem("ogt_done"), sem("ogt_evac"), sem("y_done")
        xp_ready, ln2_stats, ln2_rstd, ln2_norm = (sem(n) for n in ("xp_ready", "ln2_stats", "ln2_rstd", "ln2_norm"))
        t2_done, h2t_done, x_summed = sem("t2_done"), sem("h2t_done"), sem("x_summed")
        dve_ln1 = Chain(sem("dve_ln1_chain"), 1)
        act_ln1 = Chain(sem("act_ln1_chain"), 1)
        act_z = Chain(sem("act_z_chain"), 2)
        dve_kv = Chain(sem("dve_kv_chain"), 1)
        dve_o = Chain(sem("dve_o_chain"), 1)
        act_o = Chain(sem("act_o_chain"), 1)
        dve_ln2 = Chain(sem("dve_ln2_chain"), 1)
        act_ln2 = Chain(sem("act_ln2_chain"), 1)

        STAGES_A, FIRST_A = 6, 6

        x_tok = a["x"].rearrange("(n g p) d -> p n g d", p=P, g=4)
        x_pairs = x_sb[:, :].rearrange("p (n g d) -> p n g d", g=4, d=D)


        def four(ap):
            return ap.rearrange("p (g d) -> p g d", g=4)

        eb2 = kv[:, :, :].rearrange("p a b -> p (a b)")[:, 3 * E * D:4 * E * D]

        def pair(ap, k):
            return ap[:, bass.ds(k, 1)].rearrange("p o g d -> p (o g) d")

        weight_loads = [(packed[:, :], a["packed"]), (gk2[:, :], a["gk_w2"]), (con[:, 0:C_SEL], a["con"][:, 0:C_SEL]),
                        (con[:, C_SEL:C_END], a["con"][:, C_SEL:C_END])]
        late_loads = [(numbers[:, :], a["numbers"]), (w1[:, :], a["W1"]),
                      (w2[:, :, :], a["W2"].rearrange("(m p) d -> p m d", p=P)), (b1[:, :], a["b1"]),
                      (b2[:, :], a["b2"].unsqueeze(0).to_broadcast([P, D])), (gate_w[:, :], a["ffn_gate_w"]),
                      (gate_b[:, :], a["ffn_gate_b"].unsqueeze(0).to_broadcast([P, E]))]
        expert_loads = [(ew1[:, :].rearrange("p (e n) -> p e n", e=E), a["ffn_w1"].rearrange("e d n -> d e n")),
                        (ew2[:, :].rearrange("p (e c d) -> p (e c) d", e=E, c=HC),
                         a["ffn_w2"].rearrange("e (c p) d -> p (e c) d", p=P)),
                        (eb1[:, :], a["ffn_b1"].rearrange("e n -> (e n)").unsqueeze(0).to_broadcast([P, E * H])),
                        (eb2[:, :], a["ffn_b2"].rearrange("e n -> (e n)").unsqueeze(0).to_broadcast([P, E * D]))]
        STAGES_B = 4
        EARLY_B = PAIRS + 4

        def first_of_b(step):
            def add(k):
                if k == EARLY_B:
                    step(0, 0, lambda s: s <= 0, None)

            return add

        def rest_of_b(step):
            for k in range(1, GROUPS + STAGES_B - 1):
                step(k, k % 2, lambda s: 0 <= k - s < GROUPS, None)

        GW = GT * P
        u_t = kv[:, :, :].rearrange("p a b -> p (a b)")[:, 0:4 * 512].rearrange("p (h m n) -> p h m n", h=2, m=2)
        rows = states[:, :, :].rearrange("p a b -> p (a b)")[:, 0:2 * GW].rearrange("p (s n) -> p s n", s=2)
        x1t = states[:, :, :].rearrange("p a b -> p (a b)")[:, 2 * GW:3 * GW]
        rec = carve(row_buffers, 0, [P, 4, GT, REC])
        st3, mv3, lv3, rs3 = sb("st3", [P, GT, 6]), sb("mv3", [P, 2, GT, 2]), sb("lv3", [P, GT]), sb("rs3", [P, GT])
        shift3 = sb("shift3", [P, GT])
        logit, score, key, first_hot, tmp = (sb(n, [P, GT, E]) for n in ("logit", "score", "key", "first_hot", "tmp"))
        picked = sb("picked", [P, 2, GT, E], BF16)
        top, total, inv, top1, top2, rev1, rev2, gone, row_f = (
            sb(n, [P, GT]) for n in ("top", "total", "inv", "top1", "top2", "rev1", "rev2", "gone", "row_f"))
        row_i = sb("row_i", [P, 2, GT], I32)
        next_row = sb("next_row", [P, E])
        b_added, w1_done, gelu_done, w2_done, r_done = (sem(n) for n in ("b_added", "w1_done", "gelu_done", "w2_done", "r_done"))
        ln3_stats, ln3_rstd, ln3_norm = sem("ln3_stats"), sem("ln3_rstd"), sem("ln3_norm")
        t3_done, x1t_evac, logits_done = sem("t3_done"), sem("x1t_evac"), sem("logits_done")
        shifted, exped, picked_ready, prefix_done, rows_ready = (
            sem(n) for n in ("shifted", "exped", "picked_ready", "prefix_done", "rows_ready"))
        scattered = [sem(f"scattered{q}") for q in range(4)]
        ln3_shift = sem("ln3_shift")
        dve_ln3, act_ln3 = Chain(sem("dve_ln3_chain"), 1), Chain(sem("act_ln3_chain"), 1)
        dve_shift = Chain(sem("dve_shift_chain"), 2)
        dve_pick = Chain(sem("dve_pick_chain"), 18)
        dve_row = Chain(sem("dve_row_chain"), 3)
        rec_i = rec[:, :, :, :].bitcast(I32)

        def over_experts(ap):
            return ap.unsqueeze(2).to_broadcast([P, GT, E])

        def phase_b_pe(pe):
            def step(k, slot, live, turn):
                if k == 0:
                    pe.wait_ge(late_ld, 16 * len(late_loads))
                    for read in (ht_done, k_sb, q_sb, v_sb, gate_ready):
                        pe.wait_ge(read, PAIRS)
                    pe.wait_ge(o_squared, PAIRS - 1)
                if k == 1:
                    pe.wait_ge(h2t_done, PAIRS)
                    pe.wait_ge(xp_ready, PAIRS)
                if live(0):
                    item = k
                    for hh in range(2):
                        if item > 0 and hh == 0:
                            pe.wait_ge(gelu_done, item * 4)
                        if item > 2 and hh == 1:
                            pe.wait_ge(x1t_evac, item - 2)
                        for m in range(2):
                            pe.matmul(bank[4 * hh + m][:, :], w1[:, m * P:(m + 1) * P],
                                      h2t[:, bass.ds(item * GW + hh * 512, 512)],
                                      start=True, stop=True).then_inc(w1_done, 1)
                if live(0):
                    item = k
                    for hh in range(2):
                        pe.wait_ge(gelu_done, item * 4 + (2 * hh + 2))
                        if not (isinstance(item, int) and item == 0):
                            pe.wait_ge(r_done, item * 2 + (hh - 1))
                        for g in range(4):
                            for m in range(2):
                                ins = pe.matmul(bank[2 + hh][:, g * P:(g + 1) * P],
                                                u_t[:, hh, m, g * P:(g + 1) * P], w2[:, m, :],
                                                start=(m == 0), stop=(m == 1))
                        ins.then_inc(w2_done, 1)
                if live(2):
                    item = k - 2
                    pe.wait_ge(ln3_norm, item + 1)
                    wait_items(pe, x1t_evac, item, 1)
                    if live(0):
                        pe.wait_ge(gelu_done, k * 4 + 4)
                    for g in range(GT):
                        ins = pe.transpose(bank[4 + g // 4][:, (g % 4) * P:(g % 4 + 1) * P], rec[:, item % 4, g, 0:D], ident)
                    ins.then_inc(t3_done, 1)
                def prefix():
                    if live(3):
                        item, s = k - 3, (slot - 3) % 2
                        pe.wait_ge(picked_ready, item + 1)
                        wait_items(pe, rows_ready, item, 1)
                        hot = picked[:, s, :, :].rearrange("p g e -> p (g e)")
                        pe.matmul(bank[7][:, 0:GT * E], upper[:, :], hot, start=True, stop=False)
                        for d in range(1, GT):
                            pe.matmul(bank[7][:, d * E:GT * E], ones[:, :], hot[:, 0:(GT - d) * E], start=False,
                                      stop=(d == GT - 1))
                        for g in range(GT):
                            ins = pe.matmul(bank[7][:, GT * E:GT * E + E], ones[:, :], hot[:, g * E:(g + 1) * E],
                                            start=(g == 0), stop=(g == GT - 1))
                        ins.then_inc(prefix_done, 1)

                def logits():
                    if live(2):
                        item = k - 2
                        pe.wait_ge(x1t_evac, item + 1)
                        wait_items(pe, shifted, item, 1)
                        for g in range(GT):
                            ins = pe.matmul(bank[6][:, g * E:(g + 1) * E], x1t[:, g * P:(g + 1) * P], gate_w[:, :],
                                            start=True, stop=True)
                        ins.then_inc(logits_done, 1)

                for part in (prefix, logits) if live(0) else (logits, prefix):
                    part()

            return step

        def phase_b_act(act):
            def step(k, slot, live, turn):
                if k == 0:
                    act.wait_ge(late_ld, 16 * len(late_loads))
                    act.wait_ge(scanned, PAIRS)
                if k == 1:
                    act.wait_ge(v_out, 16 * PAIRS)
                    act.wait_ge(x_summed, PAIRS)
                    act.wait_ge(ln2_norm, PAIRS)
                if 1 < k <= GROUPS:
                    act.preload_act_table_set("natural_log_exp_and_others")
                if live(1):
                    item, s = k - 1, (slot - 1) % 2
                    act.wait_ge(ln3_stats, item + 1)
                    act_ln3.start(item)
                    act_ln3.link(act.activation(lv3[:, :], mv3[:, s, :, 1], ACT.Ln, bias=eps[:, :]))
                    act_ln3.join(act)
                    act.activation(rs3[:, :], lv3[:, :], ACT.Exp, scale=-0.5).then_inc(ln3_rstd, 1)
                    act_ln3.end()
                if live(3):
                    act.wait_ge(shifted, (k - 3) + 1)
                    act.activation(score[:, :, :], logit[:, :, :], ACT.Exp).then_inc(exped, 1)
                if live(0):
                    item = k
                    for hh in range(2):
                        for m in range(2):
                            act.wait_ge(w1_done, item * 4 + (2 * hh + m + 1))
                            if item > 0:
                                act.wait_ge(w2_done, item * 2 + (hh - 1))
                            act.activation(u_t[:, hh, m, :], bank[4 * hh + m][:, :], ACT.Gelu,
                                           bias=b1[:, m:m + 1]).then_inc(gelu_done, 1)
                    if k == 0:
                        act.preload_act_table_set("natural_log_exp_and_others")
                def normed_rows():
                    if live(1):
                        item, s, q = k - 1, (slot - 1) % 2, (k - 1) % 4
                        act.wait_ge(ln3_shift, item + 1)
                        if item >= 4:
                            act.wait_ge(scattered[q], 16 * GT * (item // 4))
                        for g in range(GT):
                            ins = act.activation(rec[:, q, g, 0:D], rows[:, s, g * P:(g + 1) * P], ACT.Identity,
                                                 bias=shift3[:, g:g + 1], scale=rs3[:, g:g + 1])
                        ins.then_inc(ln3_norm, 1)

                def transposed_rows():
                    if live(2):
                        item = k - 2
                        act.wait_ge(t3_done, item + 1)
                        wait_items(act, logits_done, item, 1)
                        act.activation(x1t[:, 0:512], bank[4][:, :], ACT.Copy)
                        act.activation(x1t[:, 512:1024], bank[5][:, :], ACT.Copy).then_inc(x1t_evac, 1)

                for part in (normed_rows, transposed_rows) if live(0) else (transposed_rows, normed_rows):
                    part()

            return step

        def phase_b_dve(dve):
            def step(k, slot, live, turn):
                if k == 0:
                    dve.wait_ge(late_ld, 16 * len(late_loads))
                    dve.wait_ge(o_done, PAIRS)
                    dve.tensor_copy(next_row[:, :], con[:, C_BASE:C_BASE + E])
                if live(3):
                    item = k - 3
                    dve_shift.start(item)
                    dve.wait_ge(logits_done, item + 1)
                    dve_shift.link(dve.tensor_tensor(logit[:, :, :], bank[6][:, 0:GT * E].rearrange("p (g e) -> p g e", e=E),
                                                     gate_b[:, :].unsqueeze(1).to_broadcast([P, GT, E]), ALU.add))
                    dve_shift.join(dve)
                    dve_shift.link(dve.tensor_reduce(top[:, :], logit[:, :, :], AX, ALU.max))
                    dve_shift.join(dve)
                    dve.tensor_tensor(logit[:, :, :], logit[:, :, :], over_experts(top[:, :]),
                                      ALU.subtract).then_inc(shifted, 1)
                    dve_shift.end()
                if live(1):
                    item, s = k - 1, (slot - 1) % 2
                    dve.wait_ge(ln3_rstd, item + 1)
                    dve.scalar_tensor_tensor(shift3[:, :], mv3[:, s, :, 0], -1.0, rs3[:, :], ALU.mult,
                                             ALU.mult).then_inc(ln3_shift, 1)
                if live(3):
                    item, s = k - 3, (slot - 3) % 2
                    c = dve_pick
                    c.start(item)

                    def then(ins):
                        c.link(ins)
                        c.join(dve)

                    dve.wait_ge(exped, item + 1)
                    then(dve.tensor_reduce(total[:, :], score[:, :, :], AX, ALU.add))
                    then(dve.reciprocal(inv[:, :], total[:, :]))
                    then(dve.tensor_tensor(score[:, :, :], score[:, :, :], over_experts(inv[:, :]), ALU.mult))
                    then(dve.tensor_reduce(top1[:, :], score[:, :, :], AX, ALU.max))
                    then(dve.tensor_tensor(key[:, :, :], score[:, :, :], over_experts(top1[:, :]), ALU.is_equal))
                    then(dve.tensor_tensor(key[:, :, :], key[:, :, :], rev, ALU.mult))
                    then(dve.tensor_reduce(rev1[:, :], key[:, :, :], AX, ALU.max))
                    then(dve.tensor_tensor(first_hot[:, :, :], rev, over_experts(rev1[:, :]), ALU.is_equal))
                    then(dve.scalar_tensor_tensor(tmp[:, :, :], first_hot[:, :, :], -2.0, score[:, :, :], ALU.mult, ALU.add))
                    then(dve.tensor_reduce(top2[:, :], tmp[:, :, :], AX, ALU.max))
                    then(dve.tensor_tensor(key[:, :, :], tmp[:, :, :], over_experts(top2[:, :]), ALU.is_equal))
                    then(dve.tensor_tensor(key[:, :, :], key[:, :, :], rev, ALU.mult))
                    then(dve.tensor_reduce(rev2[:, :], key[:, :, :], AX, ALU.max))
                    then(dve.tensor_scalar(gone[:, :], top2[:, :], 0.0, float(E), ALU.is_le, ALU.mult))
                    then(dve.tensor_tensor(rev2[:, :], rev2[:, :], gone[:, :], ALU.add))
                    then(dve.tensor_tensor(rev1[:, :], rev1[:, :], rev2[:, :], ALU.min))
                    dve.tensor_tensor(picked[:, s, :, :], rev, over_experts(rev1[:, :]), ALU.is_equal).then_inc(picked_ready, 1)
                    dve.wait_ge(picked_ready, item + 1)
                    then(dve.tensor_tensor(tmp[:, :, :], score[:, :, :], picked[:, s, :, :], ALU.mult))
                    then(dve.tensor_reduce(rec[:, item % 4, :, D], tmp[:, :, :], AX, ALU.add))
                    hold(dve)
                    dve.tensor_copy(rec_i[:, item % 4, :, D + 1], numbers[:, bass.ds(item * GT, GT)])
                    c.end()
                if live(0):
                    item, s = k, slot % 2
                    dve.wait_ge(b_added, item + 1)
                    wait_items(dve, ln3_norm, item, 2)
                    for hh in range(2):
                        dve.wait_ge(w2_done, item * 2 + (hh + 1))
                        dve.tensor_tensor(rows[:, s, hh * 512:(hh + 1) * 512], bank[2 + hh][:, :],
                                          x_sb[:, bass.ds(item * GW + hh * 512, 512)], ALU.add).then_inc(r_done, 1)
                        dve.wait_ge(r_done, item * 2 + hh + 1)
                        for g in range(4 * hh, 4 * hh + 4):
                            ins = dve.bn_stats(st3[:, g, :], rows[:, s, g * P:(g + 1) * P])
                    dve_ln3.start(item)
                    dve_ln3.link(ins)
                    dve_ln3.join(dve)
                    hold(dve)
                    for g in range(GT):
                        ins = dve.bn_aggr(mv3[:, s, g, :], st3[:, g, :])
                    ins.then_inc(ln3_stats, 1)
                    dve_ln3.end()
                if live(3):
                    item, s = k - 3, (slot - 3) % 2
                    if item >= 2:
                        dve.wait_ge(scattered[(item - 2) % 4], 16 * GT * ((item - 2) // 4 + 1))
                    dve_row.start(item)
                    dve.wait_ge(prefix_done, item + 1)
                    dve_row.link(dve.tensor_tensor(tmp[:, :, :], bank[7][:, 0:GT * E].rearrange("p (g e) -> p g e", e=E),
                                                   next_row[:, :].unsqueeze(1).to_broadcast([P, GT, E]), ALU.add))
                    dve_row.join(dve)
                    dve_row.link(dve.tensor_tensor(tmp[:, :, :], tmp[:, :, :], picked[:, s, :, :], ALU.mult))
                    dve_row.join(dve)
                    dve.tensor_tensor(next_row[:, :], next_row[:, :], bank[7][:, GT * E:GT * E + E], ALU.add)
                    dve_row.link(dve.tensor_reduce(row_f[:, :], tmp[:, :, :], AX, ALU.add))
                    dve_row.join(dve)
                    dve.tensor_copy(row_i[:, s, :], row_f[:, :]).then_inc(rows_ready, 1)
                    dve_row.end()

            return step

        def phase_b_pool(pool):
            def add_b2(item):
                pool.wait_ge(x_summed, 2 * item + 2)
                xs = x_sb[:, item * GW:(item + 1) * GW].rearrange("p (g d) -> p g d", d=D)
                pool.tensor_tensor(xs, xs, b2[:, :].unsqueeze(1).to_broadcast([P, GT, D]), ALU.add).then_inc(b_added, 1)

            def step(k, slot, live, turn):
                if k == 0:
                    pool.wait_ge(late_ld, 16 * len(late_loads))
                    add_b2(0)
                if live(-1):
                    add_b2(k + 1)
                if live(3):
                    item, q = k - 3, (k - 3) % 4
                    pool.wait_ge(rows_ready, item + 1)
                    for g in range(GT):
                        pool.indirect_dma_start(
                            out=regions,
                            out_offset=bass.IndirectOffsetOnAxis(ap=row_i[:, item % 2, g:g + 1].bitcast(U32), axis=0),
                            in_=rec[:, q, g, :], in_offset=None).then_inc(scattered[q], 16)

            return step

        STAGES_C, FIRST_C, UNROLL_C, SLOTS_C = 8, 23, 16, 8
        tab_cnt, tab_n, tab_end = (sb(n, [P, E]) for n in ("tab_cnt", "tab_n", "tab_end"))
        scratch = kv[:, :, :].rearrange("p a b -> p (a b)")
        tab_big = scratch[:, 0:E * NTILE]
        tab_ge = scratch[:, 512:512 + SLOTS * E]
        tab_mul = scratch[:, 1100:1100 + SLOTS * E]
        slot_e, slot_row, slot_start = (sb(n, [P, SLOTS]) for n in ("slot_e", "slot_row", "slot_start"))
        slot_ei, slot_rowi = sb("slot_ei", [P, SLOTS], I32), sb("slot_rowi", [P, SLOTS], I32)
        pad_i = sb("pad_i", [P, E], I32)
        pads_ready, table_ready, padded = sem("pads_ready"), sem("table_ready"), sem("padded")
        dve_tab = Chain(sem("dve_table_chain"), 13)
        at = [0]

        def over_x(shape):
            view = carve(x_sb, at[0], shape)
            at[0] += int(np.prod(shape[1:]))
            return view

        rc, xb = over_x([P, SLOTS_C, REC]), over_x([P, SLOTS_C, D])
        c_xw, c_xwt = (over_x([P, 2, D]) for _ in range(2))
        c_z = over_x([P, 4, D])
        c_y = over_x([P, SLOTS_C, D])
        c_h, c_ht = over_x([P, 2, H]), over_x([P, 2, H])
        c_id = carve(x_sb, at[0], [P, SLOTS_C], I32)
        at[0] += SLOTS_C
        c_st, c_mv, c_lv, c_rs = over_x([P, 6]), over_x([P, 4, 2]), over_x([P, 4]), over_x([P, 4])
        rc_ld, out_sc = ([sem(f"{n}{q}") for q in range(SLOTS_C)] for n in ("record_loaded", "rows_stored"))
        xw_done, xwt_done, xwt_evac, h_done, hb_done, xb_done = (
            sem(n) for n in ("xw_done", "xwt_done", "xwt_evac", "h_done", "hb_done", "xb_done"))
        htt_done, relu_done, y2_done, c_stats, c_rstd, yn_ready = (
            sem(n) for n in ("h_transposed", "relu_done", "y2_done", "c_stats", "c_rstd", "rows_normed"))
        dve_c = Chain(sem("dve_c_chain"), 2)
        act_c = Chain(sem("act_c_chain"), 1)

        def experts_of(eng):
            known = {}

            def get(k, slot, back):
                key = k - back if isinstance(k, int) else ("body", (slot - FIRST_C) % UNROLL_C - back)
                if key not in known:
                    known[key] = eng.value_load(slot_ei[0:1, bass.ds(k - back, 1)], min_val=0, max_val=E - 1)
                return known[key]

            return get

        def read_ahead(expert, k, slot, back):
            if (slot + 1 - FIRST_C) % UNROLL_C and not (isinstance(k, int) and k + 1 - back >= SLOTS):
                expert(k + 1, slot + 1, back)

        def stored_before(eng, q, turn):
            if not (isinstance(turn, int) and turn <= 0):
                eng.wait_ge(out_sc[q], turn * 16)

        def phase_c_loads(sp):
            sp.wait_ge(pads_ready, 1)
            sp.wait_ge(pad_ready, 1)
            for e in range(E):
                row = sp.value_load(pad_i[0:1, e:e + 1], min_val=0, max_val=E * REGION)
                sp.dma_start(regions[bass.ds(row, P), :], pad_record[:, :]).then_inc(padded, 16)
            sp.wait_ge(table_ready, 1)
            for q in range(4):
                sp.wait_ge(scattered[q], 16 * GT * (GROUPS // 4))
            sp.wait_ge(padded, 16 * E)
            sp.wait_ge(pad_out, 16)

            def step(k, slot, live, turn):
                if live(0):
                    wait_items(sp, xw_done, k, SLOTS_C)
                    wait_items(sp, xb_done, k, SLOTS_C)
                    row = sp.value_load(slot_rowi[0:1, bass.ds(k, 1)], min_val=0, max_val=E * REGION)
                    sp.dma_start(rc[:, slot % SLOTS_C, :], regions[bass.ds(row, P), :]).then_inc(rc_ld[slot % SLOTS_C], 16)

            pipeline(sp, SLOTS, STAGES_C, FIRST_C, UNROLL_C, step, SLOTS_C)
            for q in range(SLOTS_C):
                sp.wait_ge(out_sc[q], 16 * len(range(q, SLOTS, SLOTS_C)))

        def phase_c_pe(pe):
            pe.wait_ge(table_ready, 1)
            pe.wait_ge(e_ld, 16 * 4)

            expert = experts_of(pe)

            def step(k, slot, live, turn):
                if live(3):
                    item, s = k - 3, (slot - 3) % 2
                    e1 = expert(k, slot, 3)
                    pe.wait_ge(xwt_evac, item + 1)
                    wait_items(pe, hb_done, item, 2)
                    pe.matmul(bank[2 + s][:, :], c_xwt[:, s, :], ew1[:, bass.ds(e1 * H, H)],
                              start=True, stop=True).then_inc(h_done, 1)
                    read_ahead(expert, k, slot, 3)
                if live(5):
                    e2 = expert(k, slot, 5)
                if live(2):
                    item, s = k - 2, (slot - 2) % 2
                    pe.wait_ge(xw_done, item + 1)
                    wait_items(pe, xwt_evac, item, 2)
                    pe.transpose(bank[s][:, 0:P], c_xw[:, s, :], ident).then_inc(xwt_done, 1)
                if live(5):
                    item, s = k - 5, (slot - 5) % 2
                    pe.wait_ge(relu_done, item + 1)
                    wait_items(pe, c_stats, item, 2)
                    for c in range(HC):
                        ins = pe.matmul(bank[6 + s][:, 0:D], c_ht[:, s, c * P:(c + 1) * P],
                                        ew2[:, bass.ds(e2 * (HC * D) + c * D, D)], start=(c == 0), stop=(c == HC - 1))
                    ins.then_inc(y2_done, 1)
                if live(4):
                    item, s = k - 4, (slot - 4) % 2
                    pe.wait_ge(hb_done, item + 1)
                    wait_items(pe, relu_done, item, 2)
                    for c in range(HC):
                        ins = pe.transpose(bank[4 + s][:, c * P:(c + 1) * P], c_h[:, s, c * P:(c + 1) * P], ident)
                    ins.then_inc(htt_done, 1)

            pipeline(pe, SLOTS, STAGES_C, FIRST_C, UNROLL_C, step, SLOTS_C)

        def phase_c_act(act):
            def step(k, slot, live, turn):
                if live(5):
                    item, s = k - 5, (slot - 5) % 2
                    act.wait_ge(htt_done, item + 1)
                    wait_items(act, y2_done, item, 2)
                    act.activation(c_ht[:, s, :], bank[4 + s][:, :], ACT.Relu).then_inc(relu_done, 1)
                if live(1):
                    item, s, q = k - 1, (slot - 1) % 2, (slot - 1) % SLOTS_C
                    act.wait_ge(rc_ld[q], turn(1) * 16 + 16)
                    wait_items(act, xwt_done, item, 2)
                    act.activation(c_xw[:, s, :], rc[:, q, 0:D], ACT.Copy, scale=rc[:, q, D:D + 1]).then_inc(xw_done, 1)
                if live(7):
                    item, s = k - 7, (slot - 7) % 4
                    act.wait_ge(c_stats, item + 1)
                    act_c.start(item)
                    act_c.link(act.activation(c_lv[:, s:s + 1], c_mv[:, s, 1:2], ACT.Ln, bias=eps[:, :]))
                    act_c.join(act)
                    act.activation(c_rs[:, s:s + 1], c_lv[:, s:s + 1], ACT.Exp, scale=-0.5).then_inc(c_rstd, 1)
                    act_c.end()
                if live(2):
                    item, s = k - 2, (slot - 2) % 2
                    act.wait_ge(xwt_done, item + 1)
                    wait_items(act, h_done, item, 2)
                    act.activation(c_xwt[:, s, :], bank[s][:, 0:P], ACT.Copy).then_inc(xwt_evac, 1)

            pipeline(act, SLOTS, STAGES_C, FIRST_C, UNROLL_C, step, SLOTS_C)

        def phase_c_dve(dve):
            c = dve_tab
            c.start(0)

            def then(ins):
                c.link(ins)
                c.join(dve)

            dve.tensor_copy(pad_i[:, :], next_row[:, :]).then_inc(pads_ready, 1)
            then(dve.tensor_tensor(tab_cnt[:, :], next_row[:, :], con[:, C_BASE:C_BASE + E], ALU.subtract))
            big = tab_big.rearrange("p (e j) -> p e j", e=E)
            then(dve.tensor_tensor(big, tab_cnt[:, :].unsqueeze(2).to_broadcast([P, E, NTILE]),
                                   con[:, C_128:C_128 + NTILE].unsqueeze(1).to_broadcast([P, E, NTILE]), ALU.is_gt))
            then(dve.tensor_reduce(tab_n[:, :], big, AX, ALU.add))
            then(dve.tensor_tensor_scan(tab_end[:, :], ones[:, 0:E], tab_n[:, :], 0.0, ALU.mult, ALU.add))
            ge = tab_ge.rearrange("p (j e) -> p j e", e=E)
            mul = tab_mul.rearrange("p (j e) -> p j e", e=E)
            j3 = con[:, C_J:C_J + SLOTS].unsqueeze(2).to_broadcast([P, SLOTS, E])
            then(dve.tensor_tensor(ge, j3, tab_end[:, :].unsqueeze(1).to_broadcast([P, SLOTS, E]), ALU.is_ge))
            then(dve.tensor_reduce(slot_e[:, :], ge, AX, ALU.add))
            then(dve.tensor_tensor(mul, ge, tab_n[:, :].unsqueeze(1).to_broadcast([P, SLOTS, E]), ALU.mult))
            then(dve.tensor_reduce(slot_start[:, :], mul, AX, ALU.add))
            then(dve.tensor_tensor(slot_start[:, :], con[:, C_J:C_J + SLOTS], slot_start[:, :], ALU.subtract))
            then(dve.tensor_scalar(slot_start[:, :], slot_start[:, :], float(P), None, ALU.mult))
            then(dve.scalar_tensor_tensor(slot_row[:, :], slot_e[:, :], float(REGION), slot_start[:, :], ALU.mult, ALU.add))
            then(dve.tensor_scalar(slot_row[:, :], slot_row[:, :], float(E * REGION), None, ALU.min))
            then(dve.tensor_scalar(slot_e[:, :], slot_e[:, :], float(E - 1), None, ALU.min))
            dve.tensor_copy(slot_ei[:, :], slot_e[:, :])
            dve.tensor_copy(slot_rowi[:, :], slot_row[:, :]).then_inc(table_ready, 1)
            c.end()
            dve.wait_ge(table_ready, 1)
            dve.wait_ge(e_ld, 16 * 4)

            expert = experts_of(dve)

            def step(k, slot, live, turn):
                if live(3):
                    item, s = k - 3, (slot - 3) % 2
                    e = expert(k, slot, 3)
                    dve.wait_ge(h_done, item + 1)
                    wait_items(dve, htt_done, item, 2)
                    dve.tensor_tensor(c_h[:, s, :], bank[2 + s][:, :], eb1[:, bass.ds(e * H, H)],
                                      ALU.add).then_inc(hb_done, 1)
                    read_ahead(expert, k, slot, 3)
                if live(7):
                    item, q = k - 7, (slot - 7) % SLOTS_C
                    dve.wait_ge(c_rstd, item + 1)
                    stored_before(dve, q, turn(7))
                    dve.tensor_scalar(c_y[:, q, :], c_z[:, q % 4, :], c_mv[:, q % 4, 0:1], c_rs[:, q % 4:q % 4 + 1],
                                      ALU.subtract, ALU.mult).then_inc(yn_ready, 1)
                if live(5):
                    item, s, q = k - 5, (slot - 5) % 2, (slot - 5) % SLOTS_C
                    dve_c.start(item)
                    dve.wait_ge(y2_done, item + 1)
                    dve.wait_ge(xb_done, item + 1)
                    dve_c.link(dve.tensor_tensor(c_z[:, q % 4, :], bank[6 + s][:, 0:D], xb[:, q, :], ALU.add))
                    dve_c.join(dve)
                    dve_c.link(dve.bn_stats(c_st[:, :], c_z[:, q % 4, :]))
                    dve_c.join(dve)
                    hold(dve)
                    dve.bn_aggr(c_mv[:, q % 4, :], c_st[:, :]).then_inc(c_stats, 1)
                    dve_c.end()

            pipeline(dve, SLOTS, STAGES_C, FIRST_C, UNROLL_C, step, SLOTS_C)

        def phase_c_pool(pool):
            pool.wait_ge(table_ready, 1)
            pool.wait_ge(e_ld, 16 * 4)

            expert = experts_of(pool)

            def step(k, slot, live, turn):
                if live(1):
                    item, q = k - 1, (slot - 1) % SLOTS_C
                    e = expert(k, slot, 1)
                    pool.wait_ge(rc_ld[q], turn(1) * 16 + 16)
                    wait_items(pool, c_stats, item, SLOTS_C)
                    stored_before(pool, q, turn(1))
                    hold(pool)
                    pool.tensor_copy(c_id[:, q:q + 1], rc[:, q, D + 1:REC].bitcast(I32))
                    pool.tensor_tensor(xb[:, q, :], rc[:, q, 0:D], eb2[:, bass.ds(e * D, D)], ALU.add).then_inc(xb_done, 1)
                if live(7):
                    item, q = k - 7, (slot - 7) % SLOTS_C
                    pool.wait_ge(yn_ready, item + 1)
                    hold(pool)
                    pool.indirect_dma_start(
                        out=out, out_offset=bass.IndirectOffsetOnAxis(ap=c_id[:, q:q + 1].bitcast(U32), axis=0),
                        in_=c_y[:, q, :], in_offset=None, bounds_check=NTOK - 1, oob_is_err=False).then_inc(out_sc[q], 16)

            pipeline(pool, SLOTS, STAGES_C, FIRST_C, UNROLL_C, step, SLOTS_C)
        block = ctx.enter_context(nc.Block())

        @block.sync
        def _(sp):
            sp.dma_start(x_pairs[:, 0], x_tok[:, 0]).then_inc(x_ld, 16)
            for dst, src in weight_loads:
                sp.dma_start(dst, src).then_inc(w_ld, 16)

            def step(k, slot, live, turn):
                if live(0):
                    if not (isinstance(k, int) and k == 0):
                        sp.dma_start(pair(x_pairs, k), pair(x_tok, k)).then_inc(x_ld, 16)
                if isinstance(k, int) and k == 3:
                    for dst, src in late_loads:
                        sp.dma_start(dst, src).then_inc(late_ld, 16)
                    sp.wait_ge(pad_ready, 1)
                    sp.dma_start(regions[E * REGION:E * REGION + P, :], pad_record[:, :]).then_inc(pad_out, 16)
                if live(1):
                    item, s = k - 1, (slot - 1) % 2
                    wait_items(sp, v_in, item, 2, 16)
                    sp.wait_ge(v_sb, item + 1)
                    sp.dma_start(v_dram[s].rearrange("b h v t -> (h v) b t"),
                                 vt[:, s, :].rearrange("p (b t) -> p b t", b=2)).then_inc(v_out, 16)
                    sp.wait_ge(v_out, item * 16 + 16)
                    wait_items(sp, scanned, item, 2)
                    for b in range(2):
                        src = v_dram[s, b].rearrange("h v t -> h (v t)").unsqueeze(1).to_broadcast([HEADS, DK, DV * T])
                        sp.dma_start(kv[b * KD:(b + 1) * KD, s, :], src).then_inc(v_in, 16)

            pipeline(sp, PAIRS, STAGES_A, FIRST_A, 2, step)
            sp.wait_ge(scanned, PAIRS)
            for dst, src in expert_loads:
                sp.dma_start(dst, src).then_inc(e_ld, 16)
            phase_c_loads(sp)

        @block.tensor
        def _(pe):
            pe.wait_ge(w_ld, 16 * len(weight_loads))
            pe.transpose(bank[1][0:LOW, 0:P], gk1[:, :], ident).then_inc(setup_pe, 1)
            pe.wait_ge(setup_dve, 1)
            pe.matmul(bank[2][:, 0:KD], gk1t[:, :], gk2[:, :], start=True, stop=True).then_inc(setup_pe, 1)
            pe.wait_ge(setup_dve, SETUP)

            def step(k, slot, live, turn):
                if live(1):
                    item, s = k - 1, (slot - 1) % 2
                    pe.wait_ge(ht_done, item + 1)
                    wait_items(pe, v_sb, item, 1)
                    pe.matmul(bank[3][:, :], wv[:, :], ht[:, :], start=True, stop=True).then_inc(v_done, 1)
                if live(3):
                    item, s = k - 3, (slot - 3) % 2
                    pe.wait_ge(q_applied, item + 1)
                    wait_items(pe, o_squared, item, 1)
                    for th in range(2):
                        for v in range(DV):
                            cols = bank[5][:, :].rearrange("p (t b w n) -> p t b w n", t=2, b=2, w=2)[:, th, :, v // VL, :]
                            ins = pe.matmul(cols, states[:, s, v * T + th * P:v * T + th * P + P],
                                            sel_v[:, v % VL, :].rearrange("p (b n) -> p b n", b=2),
                                            start=(v % VL == 0), stop=(v % VL == VL - 1))
                    ins.then_inc(o_done, 1)
                if live(4):
                    item, s = k - 4, (slot - 4) % 2
                    pe.wait_ge(o_normed, item + 1)
                    wait_items(pe, ogt_evac, item, 1)
                    wait_items(pe, h2t_done, item, 2)
                    for th in range(2):
                        for b in range(2):
                            col, tok = (2 * th + b) * P, b * T + th * P
                            ins = pe.transpose(bank[6][:, tok:tok + P], og[:, s, col:col + P], ident)
                    ins.then_inc(ogt_done, 1)
                if live(1):
                    item = k - 1
                    wait_items(pe, z_parts, item, 1)
                    wait_items(pe, k_sb, item, 1)
                    for col, w in ((0, wz), (T, wk)):
                        for b in range(2):
                            ins = pe.matmul(bank[1][b * KD:(b + 1) * KD, col:col + T], w[:, :],
                                            ht[:, b * T:(b + 1) * T], start=True, stop=True)
                    ins.then_inc(zk_done, 1)
                    wait_items(pe, q_sb, item, 1)
                    for b in range(2):
                        ins = pe.matmul(bank[2][b * KD:(b + 1) * KD, 0:T], wq[:, :], ht[:, b * T:(b + 1) * T],
                                        start=True, stop=True)
                    ins.then_inc(q_done, 1)
                    wait_items(pe, gate_ready, item, 1)
                    for th in range(2):
                        for b in range(2):
                            col, tok = (2 * th + b) * P, b * T + th * P
                            ins = pe.matmul(bank[4][:, col:col + P], ht[:, tok:tok + P], wg[:, :],
                                            start=True, stop=True)
                    ins.then_inc(g_done, 1)
                def second_norm():
                    if live(5):
                        item = k - 5
                        pe.wait_ge(ln2_norm, item + 1)
                        if live(4):
                            pe.wait_ge(ogt_evac, item + 2)
                        else:
                            pe.wait_ge(h2t_done, item)
                        for g in range(4):
                            ins = pe.transpose(bank[6][:, g * P:(g + 1) * P], xn2[:, g * P:(g + 1) * P], ident)
                        ins.then_inc(t2_done, 1)

                def output_product():
                    if live(4):
                        item = k - 4
                        pe.wait_ge(ogt_evac, item + 1)
                        wait_items(pe, xp_ready, item, 1)
                        for g in range(4):
                            ins = pe.matmul(bank[7][:, g * P:(g + 1) * P], ogt[:, g * P:(g + 1) * P], wo[:, :],
                                            start=True, stop=True)
                        ins.then_inc(y_done, 1)

                for part in (second_norm, output_product) if live(1) else (output_product, second_norm):
                    part()
                if live(0):
                    item, s = k, slot % 2
                    pe.wait_ge(ln1_norm, item + 1)
                    wait_items(pe, ht_done, item, 1)
                    for g in range(4):
                        ins = pe.transpose(bank[0][:, g * P:(g + 1) * P], xn[:, s, g * P:(g + 1) * P], ident)
                    ins.then_inc(t1_done, 1)

            step_b = phase_b_pe(pe)
            pipeline(pe, PAIRS, STAGES_A, FIRST_A, 2, step, before=first_of_b(step_b))
            rest_of_b(step_b)
            phase_c_pe(pe)

        @block.scalar
        def _(act):
            act.preload_act_table_set("natural_log_exp_and_others")
            act.wait_ge(eps_ready, 2)
            act.wait_ge(w_ld, 16 * len(weight_loads))
            act.wait_ge(setup_dve, SETUP)

            def step(k, slot, live, turn):
                if live(1):
                    item, s = k - 1, (slot - 1) % 2
                    act.wait_ge(v_done, item + 1)
                    wait_items(act, v_out, item, 2, 16)
                    act.activation(vt[:, s, :], bank[3][:, :], ACT.Copy).then_inc(v_sb, 1)
                if live(2):
                    item, s = k - 2, slot % 2
                    act.wait_ge(zg_sum, item + 1)
                    act.activation(decay[:, s, :], zg_neg[:, 0:T], ACT.Exp, scale=-1.0 / 16).then_inc(decay_ready, 1)
                    wait_items(act, gate_ready, item, 1)
                    act.activation(g_sig[:, :], zg_neg[:, T:], ACT.Exp, scale=-1.0).then_inc(g_sig_ready, 1)
                if live(5):
                    item = k - 5
                    act.wait_ge(ln2_stats, item + 1)
                    act_ln2.start(item)
                    act_ln2.link(act.activation(lv2[:, :], mv2[:, :, 1], ACT.Ln, bias=eps[:, :]))
                    act_ln2.join(act)
                    act.activation(rs2[:, :], lv2[:, :], ACT.Exp, scale=-0.5).then_inc(ln2_rstd, 1)
                    act_ln2.end()
                if live(0):
                    item, s = k, slot % 2
                    act.wait_ge(ln1_stats, item + 1)
                    act_ln1.start(item)
                    act_ln1.link(act.activation(lv1[:, :], mv1[:, s, :, 1], ACT.Ln, bias=eps[:, :]))
                    act_ln1.join(act)
                    act.activation(rs1[:, s, :], lv1[:, :], ACT.Exp, scale=-0.5).then_inc(ln1_rstd, 1)
                    act_ln1.end()
                if live(3):
                    item = k - 3
                    act.wait_ge(o_done, item + 1)
                    wait_items(act, o_gated, item, 1)
                    act.activation(o_rows[:, :], bank[5][:, :], ACT.Copy).then_inc(o_evac, 1)
                    wait_items(act, o_summed, item, 1)
                    act.activation(o_sq[:, :], bank[5][:, :], ACT.Square).then_inc(o_squared, 1)
                if live(4):
                    item = k - 4
                    act.wait_ge(ogt_done, item + 1)
                    wait_items(act, y_done, item, 1)
                    act.activation(ogt[:, :], bank[6][:, :], ACT.Copy).then_inc(ogt_evac, 1)
                if live(1):
                    item, s = k - 1, (slot - 1) % 2
                    act.wait_ge(zk_done, item + 1)
                    wait_items(act, zg_sum, item, 1)
                    act.activation(zg_abs[:, 0:T], bank[1][:, 0:T], ACT.Abs, bias=gkb[:, :])
                    wait_items(act, decay_ready, item, 1)
                    act.activation(zg_neg[:, 0:T], bank[1][:, 0:T], ACT.Relu, bias=gkb_neg[:, :],
                                   scale=-1.0).then_inc(z_parts, 1)
                    wait_items(act, scanned, item, 2)
                    act.activation(keys[:, s, :], bank[1][:, T:2 * T], ACT.Copy).then_inc(k_sb, 1)
                    act.wait_ge(q_done, item + 1)
                    wait_items(act, q_applied, item, 2)
                    act.activation(queries[:, s, :], bank[2][:, 0:T], ACT.Copy, scale=DK ** -0.5).then_inc(q_sb, 1)
                if live(1):
                    item = k - 1
                    act.wait_ge(g_done, item + 1)
                    wait_items(act, g_sig_ready, item, 1)
                    act_z.start(item)
                    act.activation(zg_neg[:, T:], bank[4][:, :], ACT.Relu, scale=-1.0)
                    act_z.link(act.activation(zg_abs[:, T:], bank[4][:, :], ACT.Abs))
                if live(1):
                    item = k - 1
                    act_z.join(act)
                    act_z.link(act.activation(zg_abs[:, :], zg_abs[:, :], ACT.Exp, scale=-1.0))
                    act_z.join(act)
                    act.activation(zg_abs[:, :], zg_abs[:, :], ACT.Ln, bias=one[:, :]).then_inc(zg_logged, 1)
                    act_z.end()
                if live(0):
                    item = k
                    act.wait_ge(t1_done, item + 1)
                    wait_items(act, g_done, item, 1)
                    act.activation(ht[:, :], bank[0][:, :], ACT.Identity, bias=lnb[:, :],
                                   scale=lnw[:, :]).then_inc(ht_done, 1)
                if live(5):
                    item = k - 5
                    act.wait_ge(t2_done, item + 1)
                    hold(act)
                    act.activation(h2t[:, bass.ds(item * W4, W4)], bank[6][:, :], ACT.Identity, bias=lnb[:, :],
                                   scale=lnw[:, :]).then_inc(h2t_done, 1)
                if live(3):
                    item, s = k - 3, (slot - 3) % 2
                    act.wait_ge(o_summed, item + 1)
                    act_o.start(item)
                    act_o.link(act.activation(o_lv[:, :], o_ss[:, :], ACT.Ln, bias=eps[:, :], scale=1.0 / DV))
                    act_o.join(act)
                    wait_items(act, o_normed, item, 2)
                    act.activation(o_rs[:, s, :], o_lv[:, :], ACT.Exp, scale=-0.5).then_inc(o_rstd, 1)
                    act_o.end()

            step_b = phase_b_act(act)
            pipeline(act, PAIRS, STAGES_A, FIRST_A, 2, step, before=first_of_b(step_b))
            rest_of_b(step_b)
            phase_c_act(act)

        @block.vector
        def _(dve):
            dve.memset(eps[:, :], EPS).then_inc(eps_ready, 1)
            dve.memset(one[:, :], 1.0).then_inc(eps_ready, 1)
            dve.memset(pad_record[:, 0:D + 1], 0.0)
            dve.memset(pad_record[:, D + 1:REC].bitcast(I32), NOWHERE).then_inc(pad_ready, 1)
            dve.wait_ge(w_ld, 16 * len(weight_loads))
            dve.wait_ge(setup_pe, 1)
            dve.tensor_copy(gk1t[:, :], bank[1][0:LOW, 0:P]).then_inc(setup_dve, 1)
            dve.tensor_copy(upper[:, :], con[:, C_UP:C_UP + P])
            dve.memset(ones[:, :], 1.0)
            dve.tensor_scalar(wo[:, :], wo_raw[:, :], rmsw[:, :], None, ALU.mult).then_inc(setup_dve, 1)
            dve.tensor_scalar(gkb_neg[:, :], gkb[:, :], -1.0, None, ALU.mult).then_inc(setup_dve, 1)
            dve.wait_ge(setup_pe, 2)
            dve.tensor_copy(wz[:, :], bank[2][:, 0:KD]).then_inc(setup_dve, 1)

            def step(k, slot, live, turn):
                if live(2):
                    item, s = k - 2, (slot - 2) % 2
                    dve.wait_ge(v_in, item * 32 + 32)
                    dve.wait_ge(k_sb, item + 1)
                    dve_kv.start(item)
                    kv3 = kv[:, s, :].rearrange("p (v t) -> p v t", v=DV)
                    dve_kv.link(dve.tensor_tensor(kv3, kv3, keys[:, s, :].unsqueeze(1).to_broadcast([P, DV, T]),
                                                  ALU.mult))
                if live(5):
                    item, s = k - 5, (slot - 5) % 2
                    dve.wait_ge(y_done, item + 1)
                    wait_items(dve, x_summed, item, 2)
                    dve.tensor_tensor(xp[:, s, :], bank[7][:, :], x_sb[:, bass.ds(item * W4, W4)],
                                      ALU.add).then_inc(xp_ready, 1)
                if live(0):
                    item, s = k, slot % 2
                    dve.wait_ge(x_ld, item * 16 + 16)
                    hold(dve)
                    dve_ln1.start(item)
                    for g in range(4):
                        ins = dve.bn_stats(st[:, s, g, :], x_sb[:, bass.ds(item * W4 + g * P, P)])
                    dve_ln1.link(ins)
                if live(5):
                    item, s = k - 5, (slot - 5) % 2
                    dve.wait_ge(xp_ready, item + 1)
                    dve_ln2.start(item)
                    for g in range(4):
                        ins = dve.bn_stats(st2[:, g, :], xp[:, s, g * P:(g + 1) * P])
                    dve_ln2.link(ins)
                if live(5):
                    item = k - 5
                    dve_ln2.join(dve)
                    hold(dve)
                    for g in range(4):
                        ins = dve.bn_aggr(mv2[:, g, :], st2[:, g, :])
                    ins.then_inc(ln2_stats, 1)
                    dve_ln2.end()
                if live(0):
                    item, s = k, slot % 2
                    dve_ln1.join(dve)
                    hold(dve)
                    for g in range(4):
                        ins = dve.bn_aggr(mv1[:, s, g, :], st[:, s, g, :])
                    ins.then_inc(ln1_stats, 1)
                    dve_ln1.end()
                if live(2):
                    item, s = k - 2, slot % 2
                    dve.wait_ge(g_sig_ready, item + 1)
                    wait_items(dve, o_gated, item, 2)
                    dve.tensor_tensor(gate[:, s, :], bank[4][:, :], g_sig[:, :], ALU.mult).then_inc(gate_ready, 1)
                if live(2):
                    item, s = k - 2, (slot - 2) % 2
                    dve_kv.join(dve)
                    dve.wait_ge(decay_ready, item + 1)
                    wait_items(dve, o_done, item, 2)
                    for v in range(DV):
                        ins = dve.tensor_tensor_scan(states[:, s, v * T:(v + 1) * T], decay[:, s, :],
                                                     kv[:, s, v * T:(v + 1) * T], 0.0, ALU.mult, ALU.add)
                    ins.then_inc(scanned, 1)
                    dve_kv.end()
                if live(3):
                    item = k - 3
                    dve.wait_ge(o_squared, item + 1)
                    wait_items(dve, o_rstd, item, 1)
                    dve_o.start(item)
                    dve_o.link(dve.tensor_reduce(o_part[:, :], o_sq[:, :].rearrange("p (c v) -> p c v", v=VL), AX,
                                                 ALU.add))
                if live(5):
                    item, s = k - 5, (slot - 5) % 2
                    dve.wait_ge(ln2_rstd, item + 1)
                    wait_items(dve, t2_done, item, 1)
                    for g in range(4):
                        ins = dve.tensor_scalar(xn2[:, g * P:(g + 1) * P], xp[:, s, g * P:(g + 1) * P],
                                                mv2[:, g, 0:1], rs2[:, g:g + 1], ALU.subtract, ALU.mult)
                    ins.then_inc(ln2_norm, 1)
                if live(3):
                    item = k - 3
                    dve_o.join(dve)
                    part = o_part[:, :].rearrange("p (t w c) -> p t w c", t=4, w=2)
                    whole = o_ss[:, :].rearrange("p (t w c) -> p t w c", t=4, w=2)
                    for w in range(2):
                        ins = dve.tensor_tensor(whole[:, :, w, :], part[:, :, 0, :], part[:, :, 1, :], ALU.add)
                    ins.then_inc(o_summed, 1)
                    dve_o.end()
                if live(0):
                    item, s = k, slot % 2
                    dve.wait_ge(ln1_rstd, item + 1)
                    wait_items(dve, t1_done, item, 2)
                    for g in range(4):
                        ins = dve.tensor_scalar(xn[:, s, g * P:(g + 1) * P], x_sb[:, bass.ds(item * W4 + g * P, P)],
                                                mv1[:, s, g, 0:1], rs1[:, s, g:g + 1], ALU.subtract, ALU.mult)
                    ins.then_inc(ln1_norm, 1)

            step_b = phase_b_dve(dve)
            pipeline(dve, PAIRS, STAGES_A, FIRST_A, 2, step, after=first_of_b(step_b))
            rest_of_b(step_b)
            phase_c_dve(dve)

        @block.gpsimd
        def _(pool):
            def step(k, slot, live, turn):
                if live(4):
                    item, s = k - 4, (slot - 4) % 2
                    pool.wait_ge(o_rstd, item + 1)
                    pool.wait_ge(o_gated, item + 1)
                    hold(pool)
                    og3 = og[:, s, :].rearrange("p (c v) -> p c v", v=VL)
                    pool.tensor_tensor(og3, og3, o_rs[:, s, :].unsqueeze(2).to_broadcast([P, P, VL]),
                                       ALU.mult).then_inc(o_normed, 1)
                if live(5):
                    item, s = k - 5, (slot - 5) % 2
                    pool.wait_ge(xp_ready, item + 1)
                    hold(pool)
                    xs = x_sb[:, bass.ds(item * W4, W4)]
                    pool.tensor_tensor(xs, xs, xp[:, s, :], ALU.add).then_inc(x_summed, 1)
                if live(3):
                    item, s = k - 3, (slot - 3) % 2
                    pool.wait_ge(o_evac, item + 1)
                    pool.wait_ge(gate_ready, item + 1)
                    wait_items(pool, ogt_done, item, 2)
                    hold(pool)
                    pool.tensor_tensor(og[:, s, :], o_rows[:, :], gate[:, s, :], ALU.mult).then_inc(o_gated, 1)
                if live(2):
                    item, s = k - 2, (slot - 2) % 2
                    pool.wait_ge(q_sb, item + 1)
                    pool.wait_ge(scanned, item + 1)
                    hold(pool)
                    st3 = states[:, s, :].rearrange("p (v t) -> p v t", v=DV)
                    pool.tensor_tensor(st3, st3, queries[:, s, :].unsqueeze(1).to_broadcast([P, DV, T]),
                                       ALU.mult).then_inc(q_applied, 1)
                if live(1):
                    item = k - 1
                    pool.wait_ge(z_parts, item + 1)
                    pool.wait_ge(zg_logged, item + 1)
                    hold(pool)
                    pool.tensor_tensor(zg_neg[:, :], zg_neg[:, :], zg_abs[:, :], ALU.add).then_inc(zg_sum, 1)

            step_b = phase_b_pool(pool)
            pipeline(pool, PAIRS, STAGES_A, FIRST_A, 2, step, after=first_of_b(step_b))
            rest_of_b(step_b)
            phase_c_pool(pool)


def kernel(**inputs):
    import numpy as _np
    import concourse.bacc as _bacc
    from concourse import mybir as _mybir
    from concourse.bass_utils import run_bass_kernel_spmd as _run

    arrays = {"con": constants(), "numbers": token_numbers()}
    for name, value in inputs.items():
        v = _np.ascontiguousarray(value)
        key = name.replace("L0_attn_", "").replace("L0_ffn_", "ffn_")
        if key == "x":
            v = v.reshape(NTOK, D)
        elif key in ("ln_w", "ln_b"):
            v = v.reshape(D, 1)
        elif key == "rms_w":
            v = _np.broadcast_to(v.reshape(2, 1, VL), (2, HEADS, VL)).reshape(D, 1)
        elif key == "gk_b2":
            v = _np.broadcast_to(v.reshape(1, KD), (2, KD)).reshape(P, 1)
        elif key == "Wg":
            v = _np.ascontiguousarray(v.reshape(D, HEADS, 2, VL).transpose(0, 2, 1, 3)).reshape(D, D)
        elif key == "Wo":
            v = _np.ascontiguousarray(v.reshape(HEADS, 2, VL, D).transpose(1, 0, 2, 3)).reshape(D, D)
        elif key == "b1":
            v = _np.ascontiguousarray(v.reshape(2, P).T)
        arrays[key] = v
    arrays["packed"] = _np.concatenate([arrays.pop(n) for n in PACKED], axis=1)
    nc = _bacc.Bacc("TRN2", target_bir_lowering=False, num_devices=1)
    aps = {n: nc.dram_tensor(f"in_{n}", v.shape, _mybir.dt.from_np(v.dtype), kind="ExternalInput").ap()
           for n, v in arrays.items()}
    out = nc.dram_tensor("out_rows", (NTOK, D), _mybir.dt.float32, kind="ExternalOutput").ap()
    gla_moe(nc, aps, out)
    r = _run(nc, [{f"in_{n}": v for n, v in arrays.items()}], core_ids=[0])
    return r.results[0]["out_rows"].reshape(B, T, D)
```
